# Optimizing a Trainium2 kernel written in Bass

```python
import numpy as np
import jax
import jax.numpy as jnp

def _softmax(x, axis=-1):
    return jax.nn.softmax(x, axis=axis)

def _gelu(x):
    return jax.nn.gelu(x, approximate=True)

def _silu(x):
    return jax.nn.silu(x)

def _sigmoid(x):
    return jax.nn.sigmoid(x)

def _layernorm(x, axis=-1, eps=1e-05):
    m = jnp.mean(x, axis=axis, keepdims=True)
    v = jnp.var(x, axis=axis, keepdims=True)
    return (x - m) / jnp.sqrt(v + eps)

def _scatter_add(tgt, idx, src, axis=0):
    return tgt.at[idx].add(src)

def _segment_sum(src, seg, n):
    return jax.ops.segment_sum(src, seg, n)
kernel_name = 'mk_xattn_ffn_d2_seqx_r8_e806d7'

def setup_inputs(seed: int=0):
    np.random.seed(seed)
    _w = jnp.asarray

    def _rec_inputs():
        import jax
        import jax.numpy as jnp
        _rk = jax.random.key(seed)
        x = -0.0002928 + 1 * jax.random.normal(jax.random.fold_in(_rk, 1), (16, 64, 256), jnp.float32)
        _lenS = 64 - jax.random.randint(jax.random.fold_in(_rk, 7), (16,), 0, max(1, 64 // 4) + 1, jnp.int32)
        _lenS2 = 64 - jax.random.randint(jax.random.fold_in(_rk, 8), (16,), 0, max(1, 64 // 4) + 1, jnp.int32)
        _ctx_512P = jax.random.normal(jax.random.fold_in(_rk, 11), (16, 16, 64), jnp.float32)
        _ctx_512c = jax.random.dirichlet(jax.random.fold_in(_rk, 511), 0.3 * jnp.ones((16,), jnp.float32), (16, 64))
        _ctx_512t = jnp.einsum('bsk,bkd->bsd', _ctx_512c, _ctx_512P)
        _ctx_512t = _ctx_512t * jax.lax.rsqrt(jnp.mean(jnp.square(_ctx_512t)) + 1e-12) * 0.953939
        ctx_512 = 0.000227908 + 0.99994 * (_ctx_512t + 0.3 * jax.random.normal(jax.random.fold_in(_rk, 611), (16, 64, 64), jnp.float32))
        return (x, ctx_512)
    x, ctx_512 = _rec_inputs()

    def _L0_xattn_setup():
        import jax, jax.numpy as jnp
        import numpy as np
        B, S, L = (2, 128, 128)
        DIM_Q, H, K, D_C, D_CQ, R = (256, 16, 128, 64, 192, 64)

        def _rope_tables(seq_len, dim, dtype):
            inv_freq = 1.0 / 10000.0 ** (jnp.arange(0, dim, 2, dtype=dtype) / dim)
            t = jnp.arange(seq_len, dtype=dtype)
            freqs = t[:, None] * inv_freq[None, :]
            sin = jnp.repeat(jnp.sin(freqs), 2, axis=-1)
            cos = jnp.repeat(jnp.cos(freqs), 2, axis=-1)
            return (sin, cos)

        def _rotate_half(x):
            h = x.shape[-1] // 2
            return jnp.concatenate([-x[..., h:], x[..., :h]], axis=-1)
        key = jax.random.key(seed)
        ks = jax.random.split(key, 8)
        s_in = 1.0 / np.sqrt(DIM_Q)
        s_k = 1.0 / np.sqrt(K)
        s_cq = 1.0 / np.sqrt(D_CQ)
        s_c = 1.0 / np.sqrt(D_C)
        return {'hidden_q': jax.random.normal(ks[0], (B, S, DIM_Q), jnp.float32), 'kv_c': jax.random.normal(ks[1], (B, L, D_C), jnp.float32), 'Wq': jax.random.normal(ks[2], (H * K, DIM_Q), jnp.float32) * s_in, 'w_kc_q': jax.random.normal(ks[3], (H, K, D_CQ), jnp.float32) * s_k, 'w_kc_kv': jax.random.normal(ks[4], (H, K, D_C), jnp.float32) * s_k, 'W_qr': jax.random.normal(ks[5], (H, D_CQ, R), jnp.float32) * s_cq / np.sqrt(R), 'W_kr': jax.random.normal(ks[6], (H, D_C, R), jnp.float32) * s_c, 'Wo': jax.random.normal(ks[7], (DIM_Q, H * K), jnp.float32) * s_k}
    _L0_xattn_all = _L0_xattn_setup()
    _L0_xattn_in = {k: v for k, v in _L0_xattn_all.items() if k in ('Wq', 'w_kc_q', 'w_kc_kv', 'W_qr', 'W_kr', 'Wo')}
    del _L0_xattn_all

    def _L0_ffn_setup():
        import jax, jax.numpy as jnp
        import numpy as np
        HIDDEN = 256
        INTER = 512
        N_EXPERTS = 8
        TOPK = 2
        BATCH, SEQ = (4, 256)
        key = jax.random.key(seed)
        k1, k2, k3, k4 = jax.random.split(key, 4)
        return {'hidden_states': jax.random.normal(k1, (BATCH, SEQ, HIDDEN), dtype=jnp.float32), 'w1': jax.random.normal(k2, (N_EXPERTS, 2 * INTER, HIDDEN), dtype=jnp.float32) * 0.02, 'w2': jax.random.normal(k3, (N_EXPERTS, HIDDEN, INTER), dtype=jnp.float32) * 0.02, 'router_w': jax.random.normal(k4, (N_EXPERTS, HIDDEN), dtype=jnp.float32) * 0.02}
    _L0_ffn_all = _L0_ffn_setup()
    _L0_ffn_in = {k: v for k, v in _L0_ffn_all.items() if k in ('w1', 'w2', 'router_w')}
    del _L0_ffn_all

    def _L1_xattn_setup():
        import jax, jax.numpy as jnp
        import numpy as np
        B, S, L = (2, 128, 128)
        DIM_Q, H, K, D_C, D_CQ, R = (256, 16, 128, 64, 192, 64)

        def _rope_tables(length, dim):
            inv = 1.0 / 10000.0 ** (jnp.arange(0, dim, 2, dtype=jnp.float32) / dim)
            f = jnp.arange(length, dtype=jnp.float32)[:, None] * inv[None, :]
            sin = jnp.repeat(jnp.sin(f), 2, axis=-1)
            cos = jnp.repeat(jnp.cos(f), 2, axis=-1)
            return (sin, cos)

        def _rotate_half(x):
            half = x.shape[-1] // 2
            return jnp.concatenate([-x[..., half:], x[..., :half]], axis=-1)

        def _apply_rope(x, sin, cos):
            return x * cos + _rotate_half(x) * sin
        key = jax.random.key(seed)
        ks = jax.random.split(key, 8)
        return {'hidden_q': jax.random.normal(ks[0], (B, S, DIM_Q), jnp.float32), 'kv_c': jax.random.normal(ks[1], (B, L, D_C), jnp.float32), 'Wq': jax.random.normal(ks[2], (H * K, DIM_Q), jnp.float32) / np.sqrt(DIM_Q).astype(np.float32), 'w_kc_q': jax.random.normal(ks[3], (H, K, D_CQ), jnp.float32) / np.sqrt(K).astype(np.float32), 'w_kc_kv': jax.random.normal(ks[4], (H, K, D_C), jnp.float32) / np.sqrt(K).astype(np.float32), 'W_qr': jax.random.normal(ks[5], (H, D_CQ, R), jnp.float32) / np.float32(np.sqrt(D_CQ) * np.sqrt(R)), 'W_kr': jax.random.normal(ks[6], (H, D_C, R), jnp.float32) / np.sqrt(D_C).astype(np.float32), 'Wo': jax.random.normal(ks[7], (DIM_Q, H * K), jnp.float32) / np.sqrt(H * K).astype(np.float32)}
    _L1_xattn_all = _L1_xattn_setup()
    _L1_xattn_in = {k: v for k, v in _L1_xattn_all.items() if k in ('Wq', 'w_kc_q', 'w_kc_kv', 'W_qr', 'W_kr', 'Wo')}
    del _L1_xattn_all

    def _L1_ffn_setup():
        import jax, jax.numpy as jnp
        import numpy as np
        TOP_K = 2
        key = jax.random.key(seed)
        ks = jax.random.split(key, 4)
        G, S, F, E, H = (4, 256, 256, 8, 256)
        return {'x': jax.random.normal(ks[0], (G, S, F), dtype=jnp.float32), 'router_logits': jax.random.normal(ks[1], (F, E), dtype=jnp.float32) * 0.02, 'gating_einsum': jax.random.normal(ks[2], (E, 2, H, F), dtype=jnp.float32) * 0.02, 'linear': jax.random.normal(ks[3], (E, H, F), dtype=jnp.float32) * 0.02, 'per_expert_scale': jnp.ones((E,), dtype=jnp.float32), 'router_scale': jnp.ones((F,), dtype=jnp.float32)}
    _L1_ffn_all = _L1_ffn_setup()
    _L1_ffn_in = {k: v for k, v in _L1_ffn_all.items() if k in ('router_logits', 'gating_einsum', 'linear', 'per_expert_scale', 'router_scale')}
    del _L1_ffn_all
    return {'x': x, 'ctx_512': ctx_512, 'L0_xattn_Wq': _L0_xattn_in['Wq'], 'L0_xattn_w_kc_q': _L0_xattn_in['w_kc_q'], 'L0_xattn_w_kc_kv': _L0_xattn_in['w_kc_kv'], 'L0_xattn_W_qr': _L0_xattn_in['W_qr'], 'L0_xattn_W_kr': _L0_xattn_in['W_kr'], 'L0_xattn_Wo': _L0_xattn_in['Wo'], 'L0_ffn_w1': _L0_ffn_in['w1'], 'L0_ffn_w2': _L0_ffn_in['w2'], 'L0_ffn_router_w': _L0_ffn_in['router_w'], 'L1_xattn_Wq': _L1_xattn_in['Wq'], 'L1_xattn_w_kc_q': _L1_xattn_in['w_kc_q'], 'L1_xattn_w_kc_kv': _L1_xattn_in['w_kc_kv'], 'L1_xattn_W_qr': _L1_xattn_in['W_qr'], 'L1_xattn_W_kr': _L1_xattn_in['W_kr'], 'L1_xattn_Wo': _L1_xattn_in['Wo'], 'L1_ffn_router_logits': _L1_ffn_in['router_logits'], 'L1_ffn_gating_einsum': _L1_ffn_in['gating_einsum'], 'L1_ffn_linear': _L1_ffn_in['linear'], 'L1_ffn_per_expert_scale': _L1_ffn_in['per_expert_scale'], 'L1_ffn_router_scale': _L1_ffn_in['router_scale']}

def reference(x, ctx_512, L0_xattn_Wq, L0_xattn_w_kc_q, L0_xattn_w_kc_kv, L0_xattn_W_qr, L0_xattn_W_kr, L0_xattn_Wo, L0_ffn_w1, L0_ffn_w2, L0_ffn_router_w, L1_xattn_Wq, L1_xattn_w_kc_q, L1_xattn_w_kc_kv, L1_xattn_W_qr, L1_xattn_W_kr, L1_xattn_Wo, L1_ffn_router_logits, L1_ffn_gating_einsum, L1_ffn_linear, L1_ffn_per_expert_scale, L1_ffn_router_scale):
    import jax
    import jax.numpy as jnp

    def _L0_xattn_ref(hidden_q, kv_c, Wq, w_kc_q, w_kc_kv, W_qr, W_kr, Wo):
        import jax, jax.numpy as jnp
        import numpy as np
        B, S, L = (2, 128, 128)
        DIM_Q, H, K, D_C, D_CQ, R = (256, 16, 128, 64, 192, 64)

        def _rope_tables(seq_len, dim, dtype):
            inv_freq = 1.0 / 10000.0 ** (jnp.arange(0, dim, 2, dtype=dtype) / dim)
            t = jnp.arange(seq_len, dtype=dtype)
            freqs = t[:, None] * inv_freq[None, :]
            sin = jnp.repeat(jnp.sin(freqs), 2, axis=-1)
            cos = jnp.repeat(jnp.cos(freqs), 2, axis=-1)
            return (sin, cos)

        def _rotate_half(x):
            h = x.shape[-1] // 2
            return jnp.concatenate([-x[..., h:], x[..., :h]], axis=-1)
        b, s, _ = hidden_q.shape
        l = kv_c.shape[1]
        q_hk = (hidden_q @ Wq.T).reshape(b, s, H, K)
        q_big = jnp.einsum('bshk,hkq->bshq', q_hk, w_kc_q)
        sin, cos = _rope_tables(l, D_C, kv_c.dtype)
        kv_rope = kv_c * cos[None] + _rotate_half(kv_c) * sin[None]
        q_r = jnp.einsum('bshq,hqr->bhsr', q_big, W_qr)
        k_r = jnp.einsum('bld,hdr->bhlr', kv_rope, W_kr)
        scores = jnp.einsum('bhsr,bhlr->bhsl', q_r, k_r)
        attn = jax.nn.softmax(scores, axis=-1)
        ctx_c = jnp.einsum('bhsl,bld->bhsd', attn, kv_rope)
        ctx_lat = jnp.einsum('bhsd,hkd->bshk', ctx_c, w_kc_kv)
        out = ctx_lat.reshape(b, s, H * K) @ Wo.T
        return out

    def _L0_ffn_ref(hidden_states, w1, w2, router_w):
        import jax, jax.numpy as jnp
        import numpy as np
        HIDDEN = 256
        INTER = 512
        N_EXPERTS = 8
        TOPK = 2
        BATCH, SEQ = (4, 256)
        orig_shape = hidden_states.shape
        x = hidden_states.reshape(-1, orig_shape[-1])
        dtype = x.dtype
        logits = x @ router_w.T
        probs = jax.nn.softmax(logits.astype(jnp.float32), axis=-1)
        topk_w, sel = jax.lax.top_k(probs, TOPK)
        topk_w = topk_w.astype(dtype)
        out = jnp.zeros_like(x)
        inter = w2.shape[-1]
        for e in range(N_EXPERTS):
            w_e = jnp.sum(jnp.where(sel == e, topk_w, jnp.zeros_like(topk_w)), axis=-1)
            y = x @ w1[e].T
            gate = jax.nn.silu(y[:, :inter])
            h = y[:, inter:] * gate
            z = h @ w2[e].T
            out = out + z * w_e[:, None]
        return out.reshape(orig_shape)

    def _L1_xattn_ref(hidden_q, kv_c, Wq, w_kc_q, w_kc_kv, W_qr, W_kr, Wo):
        import jax, jax.numpy as jnp
        import numpy as np
        B, S, L = (2, 128, 128)
        DIM_Q, H, K, D_C, D_CQ, R = (256, 16, 128, 64, 192, 64)

        def _rope_tables(length, dim):
            inv = 1.0 / 10000.0 ** (jnp.arange(0, dim, 2, dtype=jnp.float32) / dim)
            f = jnp.arange(length, dtype=jnp.float32)[:, None] * inv[None, :]
            sin = jnp.repeat(jnp.sin(f), 2, axis=-1)
            cos = jnp.repeat(jnp.cos(f), 2, axis=-1)
            return (sin, cos)

        def _rotate_half(x):
            half = x.shape[-1] // 2
            return jnp.concatenate([-x[..., half:], x[..., :half]], axis=-1)

        def _apply_rope(x, sin, cos):
            return x * cos + _rotate_half(x) * sin
        Bv, Sv, _ = hidden_q.shape
        _, Lv, _ = kv_c.shape
        q_hk = (hidden_q @ Wq.T).reshape(Bv, Sv, H, K)
        q_big = jnp.einsum('bshk,hkq->bshq', q_hk, w_kc_q)
        sin_q, cos_q = _rope_tables(Sv, D_CQ)
        q_big = _apply_rope(q_big, sin_q[None, :, None, :], cos_q[None, :, None, :])
        sin_k, cos_k = _rope_tables(Lv, D_C)
        kv_r = _apply_rope(kv_c, sin_k[None], cos_k[None])
        q_r = jnp.einsum('bshq,hqr->bhsr', q_big, W_qr)
        k_r = jnp.einsum('bld,hdr->bhlr', kv_r, W_kr)
        scores = jnp.einsum('bhsr,bhlr->bhsl', q_r, k_r)
        attn = jax.nn.softmax(scores, axis=-1)
        ctx_c = jnp.einsum('bhsl,bld->bhsd', attn, kv_r)
        ctx_lat = jnp.einsum('bhsd,hkd->bhsk', ctx_c, w_kc_kv)
        ctx = ctx_lat.transpose(0, 2, 1, 3).reshape(Bv, Sv, H * K)
        return ctx @ Wo.T

    def _L1_ffn_ref(x, router_logits, gating_einsum, linear, per_expert_scale, router_scale):
        import jax, jax.numpy as jnp
        import numpy as np
        TOP_K = 2
        G, S, F = x.shape
        E = router_logits.shape[-1]
        H = linear.shape[1]
        k = TOP_K
        dtype = x.dtype
        var = jnp.mean(jnp.square(x.astype(jnp.float32)), axis=-1, keepdims=True)
        router_input = x * jax.lax.rsqrt(var + 1e-06).astype(dtype)
        root_size = jax.lax.rsqrt(jnp.array(F, dtype=dtype))
        router_input = router_input * root_size * router_scale.astype(dtype)
        logits = jnp.einsum('gsd,de->gse', router_input, router_logits.astype(dtype))
        logits32 = logits.astype(jnp.float32)
        probs = jax.nn.softmax(logits32, axis=-1)
        _, choices = jax.lax.approx_max_k(logits32, k=k)
        indicator = jax.nn.one_hot(choices, E, dtype=probs.dtype).sum(axis=-2)
        renorm = jnp.sum(indicator * probs, axis=-1, keepdims=True)
        renorm = jnp.where(renorm > 0.0, renorm, 1.0)
        weights = probs / renorm
        x_flat = x.reshape((-1, F))
        batch_size = G * S
        choices_flat = choices.ravel()
        xs_order = choices_flat.argsort()
        xs_reverse_argsort = xs_order.argsort()
        xs_indices = jnp.repeat(jnp.arange(batch_size), k)[xs_order]
        sorted_xs = x_flat[xs_indices, :]
        choices_oh = jax.nn.one_hot(choices, num_classes=E, dtype=jnp.int32)
        tokens_per_expert = jnp.sum(choices_oh, axis=(0, 1, 2))
        combine_weights = (choices_oh.astype(jnp.float32) * jnp.expand_dims(weights, axis=2)).sum(axis=-1).astype(weights.dtype)
        w_gate = jnp.transpose(gating_einsum, (0, 3, 1, 2)).reshape(E, F, 2 * H)
        gate_out = jax.lax.ragged_dot(sorted_xs, w_gate.astype(dtype), group_sizes=tokens_per_expert)
        gate_out = gate_out.reshape(gate_out.shape[0], 2, H)
        activation = jax.nn.gelu(gate_out[:, 0, :]) * gate_out[:, 1, :]
        expert_outputs = jax.lax.ragged_dot(activation, linear.astype(dtype), group_sizes=tokens_per_expert)
        expert_indices = jnp.repeat(jnp.arange(E), tokens_per_expert, total_repeat_length=expert_outputs.shape[0])
        expert_outputs = expert_outputs * per_expert_scale.astype(expert_outputs.dtype)[expert_indices, None]
        out = expert_outputs[xs_reverse_argsort].reshape((G, S, k, -1))
        out = jnp.einsum('blkd,blk->bld', out, combine_weights, preferred_element_type=out.dtype)
        return out
    x = x + _L0_xattn_ref(_layernorm(x, axis=-1), ctx_512, L0_xattn_Wq, L0_xattn_w_kc_q, L0_xattn_w_kc_kv, L0_xattn_W_qr, L0_xattn_W_kr, L0_xattn_Wo)
    x = x + _L0_ffn_ref(_layernorm(x, axis=-1), L0_ffn_w1, L0_ffn_w2, L0_ffn_router_w)
    x = x + _L1_xattn_ref(_layernorm(x, axis=-1), ctx_512, L1_xattn_Wq, L1_xattn_w_kc_q, L1_xattn_w_kc_kv, L1_xattn_W_qr, L1_xattn_W_kr, L1_xattn_Wo)
    x = x + _L1_ffn_ref(_layernorm(x, axis=-1), L1_ffn_router_logits, L1_ffn_gating_einsum, L1_ffn_linear, L1_ffn_per_expert_scale, L1_ffn_router_scale)
    return x

_drawn_inputs = setup_inputs


def setup_inputs(seed=0):
    import zlib

    import numpy as np

    out = dict(_drawn_inputs(seed))
    spreads = {'L1_ffn_per_expert_scale': (1.0, 0.6), 'L1_ffn_router_scale': (1.0, 0.6)}
    factors = {'L0_ffn_w1': 8.0,
     'L0_ffn_w2': 8.0,
     'L0_ffn_router_w': 8.0,
     'L1_ffn_router_logits': 8.0,
     'L1_ffn_gating_einsum': 8.0,
     'L1_ffn_linear': 8.0}
    for name, (base, spread) in spreads.items():
        noise = np.random.default_rng([zlib.crc32(name.encode()), seed]).standard_normal(out[name].shape)
        drawn = base * np.exp(spread * noise) if base else spread * noise
        out[name] = jnp.asarray(drawn.astype(out[name].dtype))
    for name, factor in factors.items():
        out[name] = (out[name] * factor).astype(out[name].dtype)
    return out
```

```python
from contextlib import ExitStack

import numpy as np

import concourse.bass as bass
from concourse import mybir
from concourse.alu_op_type import AluOpType as ALU

F32 = mybir.dt.float32
BF16 = mybir.dt.bfloat16
I32 = mybir.dt.int32
U32 = mybir.dt.uint32
ACT = mybir.ActivationFunctionType
AX = mybir.AxisListType.X

P = 128
NB, S = 16, 64
TOK = NB * S
TT = TOK // P
D = 256
DC = D // P
NH, HK = 16, 128
NP = NH // 2
C = 64
QW, HQ = 192, 96
NBLK = NH * HQ // P
NE, TOPK = 8, 2
NT = TOK * TOPK // P + NE - 1
F0, F1 = 512, 256
EPS = 1e-5
GELU_C = float(np.sqrt(2.0 / np.pi))


class Queue:

    def __init__(self, sem):
        self.sem, self.count, self.items = sem, 0, []

    def add(self, waits, fn, mark=True):
        self.count += mark
        self.items.append((waits, fn, self.sem if mark else None, 1))
        return (self.sem, self.count)

    def dma(self, waits, fn, sem):
        sem.count += 16
        self.items.append((waits, fn, sem.sem, 16))
        return (sem.sem, sem.count)

    def play(self, eng):
        reached = {}
        for waits, fn, sem, by in self.items:
            for s, v in waits:
                if reached.get(id(s), 0) < v:
                    eng.wait_ge(s, v)
                    reached[id(s)] = v
            ins = fn(eng)
            if sem is not None:
                ins.then_inc(sem, by)


class Counter:
    def __init__(self, sem):
        self.sem, self.count = sem, 0

    def token(self):
        return (self.sem, self.count)


def copy_on(queue, waits, out, in_):
    return queue.add(waits, lambda e: (e.copy if hasattr(e, "copy") else e.tensor_copy)(out, in_))


def build(nc, t, out):
    with ExitStack() as ctx:
        def sb(name, shape, dt=F32):
            return ctx.enter_context(nc.sbuf_tensor(name, shape, dt))

        def sem(name):
            return ctx.enter_context(nc.semaphore(name))

        def counter(name):
            return Counter(sem(name))

        sp, act, dve, pool, pe = (Queue(sem(n)) for n in ("s_sp", "s_act", "s_dve", "s_pool", "s_pe"))

        xn_dram = [nc.dram_tensor(f"xn_dram{i}", [TOK, D], F32).ap() for i in range(2)]
        ys_dram = [nc.dram_tensor(f"ys_dram{i}", [NT * P, D], F32).ap() for i in range(2)]

        X = sb("X", [P, TT, D])
        XN = sb("XN", [P, TT, D])
        VB = sb("VB", [P, NB, P])
        KT = sb("KT", [P, NB, P])
        B = sb("B", [P, NP, D])
        consts = sb("consts", [P, 3, P])
        ident, before, ones = (consts[:, i, :] for i in range(3))
        masks = sb("masks", [P, 4, P])
        ropeq = sb("ropeq", [P, 3, 4, S])
        small = sb("small", [P, 512])
        R1 = sb("R1", [P, 64 * 256])
        R2 = sb("R2", [P, 32 * 256])
        R3 = sb("R3", [P, 25 * 256])
        R4 = sb("R4", [P, 28 * 256])
        stat = sb("stat", [P, 64])
        lnst = sb("lnst", [P, TT, 10])
        PSD = [ctx.enter_context(nc.psum_tensor(f"PSD{i}", [P, 2, 512], F32)) for i in range(4)]
        bank = [PSD[i // 2][:, i % 2, :] for i in range(8)]
        free = [[] for _ in range(8)]

        def view(region, at_kb, shape, parts=P, p0=0):
            n = int(np.prod(shape))
            v = region[p0:p0 + parts, at_kb * 256:at_kb * 256 + n]
            if len(shape) == 1:
                return v
            names = "abcd"[:len(shape)]
            return v.rearrange(f"p ({' '.join(names)}) -> p {' '.join(names)}",
                               **{k: s for k, s in zip(names[1:], shape[1:])})

        def load(name, dst, src, waits=()):
            return sp.dma(list(waits), lambda e: e.dma_start(dst, src), counter(name))

        qr0, kr0 = view(R1, 0, [2, 8, HQ]), view(R1, 6, [8, C])
        kcq0 = view(R1, 8, [2, NH, HK], parts=HQ)
        wq0, ckv0, wo0 = view(R1, 24, [NH, D]), view(R1, 40, [NH, C]), view(R1, 44, [NH, D])
        ctx_in = view(R3, 0, [NB, C])
        ctx_rope = view(R3, 4, [2, C])
        ctx_cos = view(R3, 5, [NB, C])
        ctx_sin = view(R3, 9, [NB, C])
        rout = sb("rout", [P, 2, DC, NE])
        rscale = sb("rscale", [P, DC])
        pes = sb("pes", [P, NE])
        ld_x, ld_kcq0, ld_wq0 = [], [], []
        ld_qr0 = load("ld_qr0", qr0, t["qr0"])
        ld_kr0 = load("ld_kr0", kr0, t["kr0"])
        for i in range(2):
            hs = slice(8 * i, 8 * i + 8)
            ld_x.append(load(f"ld_x{i}", X[:, 4 * i:4 * i + 4, :], t["x"][:, 4 * i:4 * i + 4, :]))
            if i == 0:
                ld_c = load("ld_consts", consts[:, :, :], t["consts"])
            ld_kcq0.append(load(f"ld_kcq0_{i}", kcq0[:, :, hs, :], t["kcq0"][:, :, hs, :]))
            ld_wq0.append(load(f"ld_wq0_{i}", wq0[:, hs, :], t["wq0"][:, hs, :]))
        ld_ctx = sp.dma([], lambda e: e.dma_start(ctx_in[0:64], t["ctx"]), counter("ld_ctx0"))
        ld_ctx2 = sp.dma([], lambda e: e.dma_start(ctx_in[64:128], t["ctx"]), counter("ld_ctx1"))
        ld_rk = load("ld_ropek", ctx_rope, t["ropek"])
        ld_ckv0 = load("ld_ckv0", ckv0, t["ckv0"])
        ld_wo0 = load("ld_wo0", wo0, t["wo0"])
        ld_small = load("ld_small", small[:, :], t["small"])
        ld_rout = load("ld_rout", rout[:, :, :, :], t["rout"])
        ld_rs = load("ld_rscale", rscale[:, :], t["rscale"])
        ld_pes = load("ld_pes", pes[:, :], t["pes"])
        ld_masks = load("ld_masks", masks[:, :, :], t["masks"])
        ld_ropeq = load("ld_ropeq", ropeq[:, :, :, :], t["ropeq"])

        half_neg = stat[:, 0:1]
        z_half = pool.add([], lambda e: e.memset(half_neg, -0.5))

        def norm_stats(tile, waits):
            bn, mv, ve = lnst[:, tile, 0:6], lnst[:, tile, 6:8], lnst[:, tile, 8:9]
            a = dve.add(list(waits), lambda e: e.bn_stats(bn, X[:, tile, :]))
            a = dve.add([a], lambda e: e.bn_aggr(mv, bn))
            a = dve.add([a], lambda e: e.tensor_scalar(ve, mv[:, 1:2], EPS, None, ALU.add))
            return pool.add([a, z_half], lambda e: e.tensor_tensor(lnst[:, tile, 9:10], ve, half_neg, ALU.pow))

        def norm_apply(tile, stats, waits=()):
            return dve.add([stats, *waits], lambda e: e.tensor_scalar(
                XN[:, tile, :], X[:, tile, :], lnst[:, tile, 6:7], lnst[:, tile, 9:10], ALU.subtract, ALU.mult))

        def transpose_xn(tile, xnT, b, xn_ready, eng, waits=()):
            for dc in range(DC):
                tr = pe.add([xn_ready, ld_c, *free[b]], lambda e, dc=dc: e.transpose(
                    bank[b][:, dc * P:(dc + 1) * P], XN[:, tile, dc * P:(dc + 1) * P], ident), mark=dc == DC - 1)
            done = copy_on(eng, [tr, *waits], xnT[:, :, tile * P:(tile + 1) * P],
                           bank[b][:, 0:DC * P].rearrange("p (a b) -> p a b", a=DC))
            free[b] = [done]
            return done

        H2 = C // 2

        def bc(ap, n):
            return ap.unsqueeze(1).to_broadcast([ap.shape[0], n, ap.shape[1]])

        zv = pool.add([], lambda e: e.memset(VB[:, :, :], 0.0))

        xnT = view(R4, 0, [DC, TOK])
        T1 = view(R3, 13, [2, NH, C], parts=HQ)
        T2 = view(R3, 21, [NH, C])
        A = view(R4, 8, [DC, NH * C])
        t1_ready, t2_ready, a_ready, xnT_ready = {}, {}, {}, []

        def first_products(hh):
            for c in range(2):
                bk = 2 + 2 * hh + c
                rows = slice(64 * hh, 64 * hh + 64)
                for h8 in range(8):
                    mm = pe.add([ld_qr0, ld_kr0, *free[bk]], lambda e, bk=bk, h8=h8, c=c, rows=rows: e.matmul(
                        bank[bk][0:HQ, h8 * C:(h8 + 1) * C], qr0[rows, c, h8, :], kr0[rows, h8, :],
                        start=True, stop=True), mark=h8 == 7)
                tk = copy_on(act, [mm], T1[:, c, 8 * hh:8 * hh + 8, :],
                             bank[bk][0:HQ, :].rearrange("p (a b) -> p a b", a=8))
                free[bk] = [tk]
                t1_ready[hh, c] = tk

        def second_products(hh):
            bk = hh
            for h8 in range(8):
                h = 8 * hh + h8
                for c in range(2):
                    mm = pe.add([ld_kcq0[hh], t1_ready[hh, 0], t1_ready[hh, 1], *free[bk]],
                                lambda e, bk=bk, h=h, h8=h8, c=c: e.matmul(
                                    bank[bk][:, h8 * C:(h8 + 1) * C], kcq0[:, c, h, :], T1[:, c, h, :],
                                    start=(c == 0), stop=(c == 1)), mark=(h8 == 7 and c == 1))
            tk = copy_on(act, [mm], T2[:, 8 * hh:8 * hh + 8, :], bank[bk].rearrange("p (a b) -> p a b", a=8))
            free[bk] = [tk]
            t2_ready[hh] = tk

        def third_products(hh):
            for dc in range(DC):
                bk = 2 + 2 * dc + hh
                for h8 in range(8):
                    h = 8 * hh + h8
                    mm = pe.add([ld_wq0[hh], t2_ready[hh], *free[bk]], lambda e, bk=bk, h=h, h8=h8, dc=dc: e.matmul(
                        bank[bk][:, h8 * C:(h8 + 1) * C], wq0[:, h, dc * P:(dc + 1) * P], T2[:, h, :],
                        start=True, stop=True), mark=h8 == 7)
                tk = copy_on(dve if dc else act, [mm], A[:, dc, 512 * hh:512 * hh + 512], bank[bk])
                free[bk] = [tk]
                a_ready[hh, dc] = tk

        def first_norm(tiles):
            stats = [norm_stats(i, [ld_x[i // 4]]) for i in tiles]
            normed = [norm_apply(i, s_) for i, s_ in zip(tiles, stats)]
            for i, xn in zip(tiles, normed):
                xnT_ready.append(transpose_xn(i, xnT, 6 + i % 2, xn, dve if i % 2 else act))

        first_products(0)
        first_products(1)
        first_norm(range(4))
        second_products(0)
        third_products(0)
        second_products(1)
        first_norm(range(4, 8))

        a = dve.add([ld_ctx, ld_ctx2, ld_rk], lambda e: e.tensor_tensor(
            ctx_cos, ctx_in, bc(ctx_rope[:, 0, :], NB), ALU.mult))
        b_ = dve.add([], lambda e: e.tensor_tensor(ctx_sin[:, :, 0:H2], ctx_in[:, :, H2:C],
                                                   bc(ctx_rope[:, 1, 0:H2], NB), ALU.mult))
        b_ = dve.add([], lambda e: e.tensor_tensor(ctx_sin[:, :, H2:C], ctx_in[:, :, 0:H2],
                                                   bc(ctx_rope[:, 1, H2:C], NB), ALU.mult))
        for par in range(2):
            h = slice(64 * par, 64 * par + 64)
            vb_ready = dve.add([b_, zv], lambda e, h=h: e.tensor_tensor(
                VB[h, :, h], ctx_cos[h], ctx_sin[h], ALU.add))
        kt_ready = []

        def turn_context():
            for i in range(4):
                bk = 6 + i % 2
                for j in range(4):
                    tr = pe.add([vb_ready, *free[bk]], lambda e, bk=bk, i=i, j=j: e.transpose(
                        bank[bk][:, j * P:(j + 1) * P], VB[:, 4 * i + j, :], ident), mark=j == 3)
                tk = copy_on(act if i % 2 else dve, [tr], KT[:, 4 * i:4 * i + 4, :],
                             bank[bk].rearrange("p (a b) -> p a b", a=4))
                free[bk] = [tk]
                kt_ready.append(tk)

        def output_matrices(ckv, wo, waits, b_waits):
            toks = []
            for i in range(4):
                bk = 2 + i
                for p2 in range(2):
                    for par in range(2):
                        h = 4 * i + 2 * p2 + par
                        mm = pe.add([*waits, *free[bk]], lambda e, bk=bk, h=h, p2=p2, par=par: e.matmul(
                            bank[bk][64 * par:64 * par + 64, p2 * D:(p2 + 1) * D], ckv[:, h, :], wo[:, h, :],
                            start=True, stop=True), mark=(p2 == 1 and par == 1))
                tk = copy_on(act if i % 2 else dve, [mm, *b_waits], B[:, 2 * i:2 * i + 2, :],
                             bank[bk].rearrange("p (a b) -> p a b", a=2))
                free[bk] = [tk]
                toks.append(tk)
            return toks, mm

        Q = view(R2, 0, [2, NP, TOK // 2])
        q_ready = {}
        turn_q = [0]

        def latent_queries0(hf, hh):
            toks = []
            for p in range(4 * hh, 4 * hh + 4):
                bk = turn_q[0] % 4
                turn_q[0] += 1
                for dc in range(DC):
                    mm = pe.add([a_ready[hh, 0], a_ready[hh, 1], *xnT_ready[4 * hf:4 * hf + 4], *free[bk]],
                                lambda e, bk=bk, p=p, hf=hf, dc=dc: e.matmul(
                                    bank[bk], A[:, dc, p * P:(p + 1) * P], xnT[:, dc, hf * 512:(hf + 1) * 512],
                                    start=(dc == 0), stop=(dc == DC - 1)), mark=dc == DC - 1)
                toks.append(copy_on(act if p % 2 else dve, [mm], Q[:, hf, p, :], bank[bk]))
                free[bk] = [toks[-1]]
            q_ready[hf, hh] = toks

        latent_queries0(0, 0)
        third_products(1)
        latent_queries0(0, 1)
        turn_context()

        class Attention:

            def __init__(self, q_ready, r3_free):
                self.q_ready = q_ready
                self.E = [view(R3, 4 * i, [NH, S]) for i in range(2)]
                self.ET = [view(R3, 8 + 4 * i, [NP, P]) for i in range(2)]
                self.CT = [view(R3, 16 + 4 * i, [NP, P]) for i in range(2)]
                self.mx, self.sm, self.rs = ([sbm[:, 32 * k + 16 * i:32 * k + 16 * i + 16] for i in range(2)]
                                             for k in range(3))
                self.e_free = [list(r3_free), list(r3_free)]
                self.et_free = [list(r3_free), list(r3_free)]
                self.ct_free = [list(r3_free), list(r3_free)]
                self.turn = 0
                self.e, self.sub, self.et, self.ct, self.q_done = {}, {}, {}, {}, {}

            def pair(self):
                k = self.turn % 4
                self.turn += 1
                return k, [*free[2 * k], *free[2 * k + 1]]

            def scores(self, i):
                k, k_free = self.pair()
                for p in range(NP):
                    for b2 in range(2):
                        b = 2 * i + b2
                        mm = pe.add([*self.q_ready(i), *kt_ready, *k_free], lambda e, p=p, b=b, b2=b2: e.matmul(
                            bank[2 * k + p // 4][64 * b2:64 * b2 + 64, (p % 4) * P:(p % 4 + 1) * P],
                            Q[:, i // 4, p, (b % 8) * S:(b % 8 + 1) * S], KT[:, b, :], start=True, stop=True),
                            mark=(p == NP - 1 and b2 == 1))
                self.q_done[i] = mm
                E, mx = self.E[i % 2], self.mx[i % 2]
                ps = PSD[k][:, :, :].rearrange("p a (h l) -> p (a h) l", l=S)
                m = dve.add([mm, *self.e_free[i % 2]], lambda e: e.tensor_reduce(mx, ps, AX, ALU.max))
                self.sub[i] = dve.add([m], lambda e: e.tensor_tensor(
                    E, ps, mx.unsqueeze(2).to_broadcast([P, NH, S]), ALU.subtract))
                free[2 * k] = free[2 * k + 1] = [self.sub[i]]

            def exponential(self, i):
                E = self.E[i % 2]
                self.e[i] = act.add([self.sub[i]], lambda e: e.activation(E, E, ACT.Exp))

            def normalise(self, i):
                E, sm, rs = self.E[i % 2], self.sm[i % 2], self.rs[i % 2]
                s = dve.add([self.e[i]], lambda e: e.tensor_reduce(sm, E, AX, ALU.add))
                s = dve.add([s], lambda e: e.reciprocal(rs, sm))
                self.e[i] = pool.add([s], lambda e: e.tensor_tensor(
                    E, E, rs.unsqueeze(2).to_broadcast([P, NH, S]), ALU.mult))

            def turn_weights(self, i):
                (k, k_free), j = self.pair(), i % 2
                for p in range(NP):
                    tr = pe.add([self.e[i], *k_free], lambda e, p=p: e.transpose(
                        bank[2 * k + p // 4][:, (p % 4) * P:(p % 4 + 1) * P],
                        self.E[j][:, 2 * p:2 * p + 2, :].rearrange("p a b -> p (a b)"), ident), mark=p == NP - 1)
                self.e_free[j] = [tr]
                self.et[i] = copy_on(act, [tr, *self.et_free[j]], self.ET[j],
                                     PSD[k][:, :, :].rearrange("p a (h l) -> p (a h) l", l=P))
                free[2 * k] = free[2 * k + 1] = [self.et[i]]

            def weighted_context(self, i):
                (k, k_free), j = self.pair(), i % 2
                self.ct[i] = []
                for b2 in range(2):
                    mm = pe.add([self.et[i], *k_free], lambda e, b2=b2: e.matmul(
                        bank[2 * k + b2], VB[:, 2 * i + b2, :], self.ET[j][:, :, b2 * S:(b2 + 1) * S],
                        start=True, stop=True))
                    tk = copy_on(act if b2 else dve, [mm, *self.ct_free[j]], self.CT[j][:, :, b2 * S:(b2 + 1) * S],
                                 bank[2 * k + b2].rearrange("p (a b) -> p a b", b=S))
                    free[2 * k + b2] = [tk]
                    self.ct[i].append(tk)
                self.et_free[j] = [mm]

            def project(self, i, b_ready, finish):
                (k, k_free), j = self.pair(), i % 2
                for p in range(NP):
                    mm = pe.add([*self.ct[i], *b_ready, *k_free], lambda e, p=p: e.matmul(
                        bank[2 * k][:, 0:D], self.CT[j][:, p, :], B[:, p, :], start=(p == 0), stop=(p == NP - 1)),
                        mark=p == NP - 1)
                self.ct_free[j] = [mm]
                self.b_done = mm
                tk = dve.add([mm], lambda e: e.tensor_tensor(X[:, i, :], bank[2 * k][:, 0:D], X[:, i, :], ALU.add))
                free[2 * k] = [tk]
                finish(i, tk)

            def run(self, b_ready, finish, apply, route, each=lambda i: None):
                for i in range(TT + 3):
                    if i < TT:
                        self.turn_weights(i)
                    if i + 2 < TT:
                        self.scores(i + 2)
                        self.exponential(i + 2)
                        each(i + 2)
                    if 0 <= i - 2 < TT:
                        apply(i - 2)
                    if i < TT:
                        self.weighted_context(i)
                    if i + 2 < TT:
                        self.normalise(i + 2)
                    if 0 <= i - 1 < TT:
                        self.project(i - 1, b_ready, finish)
                    if 0 <= i - 3 < TT:
                        route(i - 3)

        sbm = sb("sbm", [P, 96])

        at0 = Attention(lambda i: [*q_ready[i // 4, 0], *q_ready[i // 4, 1]],
                        [a_ready[1, 0], a_ready[1, 1], vb_ready])
        at0.scores(0)
        at0.exponential(0)
        latent_queries0(1, 0)
        at0.normalise(0)
        latent_queries0(1, 1)
        q0_last_mm = (pe.sem, pe.count)
        at0.scores(1)
        at0.exponential(1)
        b_ready, raw0_done = output_matrices(ckv0, wo0, [ld_ckv0, ld_wo0], [])
        at0.normalise(1)

        w1 = view(R1, 0, [DC, NE, 2 * F0])
        ld_w1 = [load(f"ld_w1_{i}", w1[:, i, :, :], t["w1"][:, i, :, :], [raw0_done]) for i in range(DC)]

        io_e, io_r = small[:, 0:8], small[:, 8:136]
        tile_of = small[:, 136:152]
        tri_e = small[:, 152:216].rearrange("p (a b) -> p a b", a=NE)
        io_g, pid = small[:, 216:216 + NT], small[:, 248:249]
        rout1_ready = [dve.add([ld_rs, ld_rout], lambda e, dc=dc: e.tensor_scalar(
            rout[:, 1, dc, :], rout[:, 1, dc, :], rscale[:, dc:dc + 1], None, ALU.mult)) for dc in range(DC)]

        LG = sb("LG", [P, TT, NE])
        VAL = sb("VAL", [P, TT, 8])
        IDX = sb("IDX", [P, TT, 8], U32)
        RT = view(R3, 14, [1024])
        RTI = sb("RTI", [P, 96], I32)
        OHR = R3[:, 18 * 256:22 * 256].bitcast(BF16).rearrange("p (a b) -> p a b", b=P)
        OHG = R3[:, 22 * 256:22 * 256 + 3 * TOPK * TT * NT // 2].bitcast(BF16).rearrange(
            "p (v a b) -> p v a b", v=3, b=NT)
        tok_of = sb("tok_of", [P, NT], I32)
        slot_of = sb("slot_of", [P, TOPK * TT], I32)
        exp_of = sb("exp_of", [P, NT], I32)
        wts = sb("wts", [P, TOPK, TT])
        rms = sb("rms", [P, 3 * TT])

        def route_tile(layer, i, xn_ready, xnT_done, rt):
            bk = 1 if i % 2 == 0 else 7
            for dc in range(DC):
                mm = pe.add([xnT_done, ld_rout, *rout1_ready, *free[bk]], lambda e, dc=dc: e.matmul(
                    bank[bk][:, 0:NE], rt_xnT[:, dc, i * P:(i + 1) * P], rout[:, layer, dc, :],
                    start=(dc == 0), stop=(dc == DC - 1)), mark=dc == DC - 1)
            if layer == 0:
                lg = dve.add([mm, *rt["lg_free"]], lambda e: e.tensor_copy(LG[:, i, :], bank[bk][:, 0:NE]))
            else:
                ms, me, mr = (rms[:, n * TT + i:n * TT + i + 1] for n in range(3))
                junk = view(R3, 24, [D])
                a = act.add([xn_ready, *rt["junk_free"]], lambda e: e.activation(
                    junk, XN[:, i, :], ACT.Square, accum_out=ms))
                rt["junk_free"] = [a]
                a = dve.add([a], lambda e: e.tensor_scalar(me, ms, 1.0 / D, 1e-6, ALU.mult, ALU.add))
                a = pool.add([a], lambda e: e.tensor_tensor(mr, me, half_neg, ALU.pow))
                lg = dve.add([a, mm, *rt["lg_free"]], lambda e: e.tensor_scalar(
                    LG[:, i, :], bank[bk][:, 0:NE], mr, float(D) ** -0.5, ALU.mult, ALU.mult))
            free[bk] = [lg]
            v = dve.add([lg], lambda e: e.max(VAL[:, i, :], LG[:, i, :]))
            rt["sorted"] = dve.add([v], lambda e: e.max_index(IDX[:, i, :], VAL[:, i, :], LG[:, i, :]))

        rt_xnT = xnT

        def route(layer, srt):
            n = [0]

            def take(k):
                v = RT[:, n[0]:n[0] + k]
                n[0] += k
                return v

            KT_ = TOPK * TT
            ev, ssum, srec = take(64).rearrange("p (a b) -> p a b", a=TT), take(8), take(8)
            w = dve.add([srt], lambda e: e.tensor_tensor(
                ev, VAL[:, :, :], VAL[:, :, 0:1].to_broadcast([P, TT, 8]), ALU.subtract))
            w = act.add([w], lambda e: e.activation(ev, ev, ACT.Exp))
            idf = take(KT_).rearrange("p (a b) -> p a b", a=TOPK)
            oh = take(KT_ * NE)
            oh3 = oh.rearrange("p (a b) -> p a b", b=NE)
            m = take(64)
            for k in range(TOPK):
                a = dve.add([], lambda e, k=k: e.tensor_copy(idf[:, k, :], IDX[:, :, k]))
            a = dve.add([a, ld_small], lambda e: e.tensor_tensor(
                oh3, bc(io_e, KT_), idf.rearrange("p a b -> p (a b)").unsqueeze(2).to_broadcast([P, KT_, NE]),
                ALU.is_equal))
            a = dve.add([a], lambda e: e.tensor_tensor(m, oh[:, 0:64], oh[:, 64:128], ALU.add))
            rank_bank = 0
            pe.add([a, *free[rank_bank]], lambda e: e.matmul(bank[rank_bank][:, 0:64], before, m, start=True, stop=False,
                                                      skip_group_check=True), mark=False)
            for i in range(TT):
                mm = pe.add([], lambda e, i=i: e.matmul(
                    bank[rank_bank][:, 8 * (i + 1):8 * (TT + 1)].rearrange("p (a b) -> p a b", b=NE), ones,
                    bc(m[:, 8 * i:8 * i + 8], TT - i), start=False, stop=(i == TT - 1),
                    skip_group_check=True), mark=i == TT - 1)
            rank = take(72)
            r = dve.add([mm], lambda e: e.tensor_copy(rank, bank[rank_bank][:, 0:72]))
            free[rank_bank] = [r]
            cnt_i, nt_f, prod = RTI[:, 0:8], take(8), take(64).rearrange("p (a b) -> p a b", a=NE)
            first, last, base = take(8), take(8), take(64).rearrange("p (a b) -> p a b", a=TT)
            a = dve.add([r], lambda e: e.tensor_scalar(cnt_i, rank[:, 64:72], float(P - 1), None, ALU.add))
            a = dve.add([a], lambda e: e.tensor_scalar(cnt_i, cnt_i, 7, None, ALU.logical_shift_right))
            a = dve.add([a], lambda e: e.tensor_copy(nt_f, cnt_i))
            a = dve.add([a], lambda e: e.tensor_tensor(prod, tri_e, bc(nt_f, NE), ALU.mult))
            a = dve.add([a], lambda e: e.tensor_reduce(first, prod, AX, ALU.add))
            a = dve.add([a], lambda e: e.tensor_tensor(last, first, nt_f, ALU.add))
            a1 = dve.add([], lambda e: e.scalar_tensor_tensor(
                base, bc(first, TT), float(P), rank[:, 0:64].rearrange("p (a b) -> p a b", a=TT),
                ALU.mult, ALU.add))
            sel, slot_f = take(KT_ * NE), take(KT_)
            a1 = dve.add([a1], lambda e: e.tensor_tensor(
                sel.rearrange("p (k x) -> p k x", k=TOPK), oh.rearrange("p (k x) -> p k x", k=TOPK),
                bc(base.rearrange("p a b -> p (a b)"), TOPK), ALU.mult))
            a1 = dve.add([a1], lambda e: e.tensor_reduce(slot_f, sel.rearrange("p (a b) -> p a b", b=NE), AX, ALU.add))
            slot_done = dve.add([a1], lambda e: e.tensor_copy(slot_of[:, :], slot_f))
            g_i, r_i, g_f, r_f = RTI[:, 8:24], RTI[:, 24:40], take(KT_), take(KT_)
            g = dve.add([slot_done], lambda e: e.tensor_scalar(g_i, slot_of[:, :], 7, None, ALU.logical_shift_right))
            r2 = dve.add([], lambda e: e.tensor_scalar(r_i, slot_of[:, :], P - 1, None, ALU.bitwise_and))
            g = dve.add([g], lambda e: e.tensor_copy(g_f, g_i))
            r2 = dve.add([r2], lambda e: e.tensor_copy(r_f, r_i))
            o1 = dve.add([g], lambda e: e.tensor_tensor(
                OHG[:, 0, :, :], bc(io_g, KT_), g_f.unsqueeze(2).to_broadcast([P, KT_, NT]), ALU.is_equal))
            dve.add([o1], lambda e: e.tensor_scalar(OHG[:, 1, :, :], OHG[:, 0, :, :], pid, None, ALU.mult))
            o2 = dve.add([], lambda e: e.tensor_tensor(
                OHG[:, 2, :, :], OHG[:, 0, :, :], tile_of.unsqueeze(2).to_broadcast([P, KT_, NT]), ALU.mult))
            o3 = dve.add([r2], lambda e: e.tensor_tensor(
                OHR[:, :, :], bc(io_r, KT_), r_f.unsqueeze(2).to_broadcast([P, KT_, P]), ALU.is_equal))
            tok_bank = 4
            for c in range(KT_):
                mm = pe.add([o2, o3, *free[tok_bank]], lambda e, c=c: e.matmul(
                    bank[tok_bank][:, 0:2 * NT].rearrange("p (a b) -> p a b", a=2), OHR[:, c, :], OHG[:, 1:3, c, :],
                    start=(c == 0), stop=(c == KT_ - 1)), mark=c == KT_ - 1)
            ge, ex_f = take(NT * NE).rearrange("p (a b) -> p a b", b=NE), take(NT)
            x = dve.add([a], lambda e: e.tensor_tensor(
                ge, io_g.unsqueeze(2).to_broadcast([P, NT, NE]), bc(last, NT), ALU.is_ge))
            x = dve.add([x], lambda e: e.tensor_reduce(ex_f, ge, AX, ALU.add))
            ex_done = dve.add([x, *rt_free["exp"]], lambda e: e.tensor_scalar(exp_of[:, :], ex_f, float(NE - 1), None, ALU.min))
            tk = take(2 * NT)
            y = dve.add([mm], lambda e: e.tensor_copy(tk, bank[tok_bank][:, 0:2 * NT]))
            free[tok_bank] = [y]
            tok_done = dve.add([y], lambda e: e.scalar_tensor_tensor(
                tok_of[:, :], tk[:, NT:2 * NT], float(P), tk[:, 0:NT], ALU.mult, ALU.add))
            s = dve.add([w], lambda e: e.tensor_reduce(ssum, ev, AX, ALU.add))
            s = dve.add([s], lambda e: e.reciprocal(srec, ssum))
            for k in range(TOPK):
                s1 = dve.add([s], lambda e, k=k: e.tensor_tensor(wts[:, k, :], ev[:, :, k], srec, ALU.mult))
            s = s1
            if layer == 1:
                ren, rec = take(8), take(8)
                s = dve.add([s], lambda e: e.tensor_tensor(ren, wts[:, 0, :], wts[:, 1, :], ALU.add))
                s = dve.add([s], lambda e: e.reciprocal(rec, ren))
                s = dve.add([s], lambda e: e.tensor_tensor(wts[:, :, :], wts[:, :, :], bc(rec, TOPK), ALU.mult))
                ps_, pk = sel.rearrange("p (a b) -> p a b", b=NE), slot_f
                s2 = dve.add([slot_done, ld_pes], lambda e: e.tensor_tensor(ps_, oh3, bc(pes[:, :], KT_), ALU.mult))
                s2 = dve.add([s2], lambda e: e.tensor_reduce(pk, ps_, AX, ALU.add))
                s = dve.add([s, s2], lambda e: e.tensor_tensor(
                    wts[:, :, :], wts[:, :, :], pk.rearrange("p (a b) -> p a b", a=TOPK), ALU.mult))
            return tok_done, ex_done, slot_done, s

        rt_free = {"exp": []}

        GX = [sb(f"GX{i}", [P, D]) for i in range(3)]
        gx_sem = [[counter(f"gx{l}_{i}") for i in range(3)] for l in range(2)]
        z_sem = [[counter(f"z{l}_{i}") for i in range(2)] for l in range(2)]

        def experts(layer, W1, W2, F, w1_ready, w2_ready, stored, tok_done, ex_done, r3_free, during=lambda: None):
            IC = F // P
            st = {}
            AH = 2 if layer else 1
            NH_ = AH + 1
            KB = F * 4 // 1024
            xsT = [view(R3, i, [DC, P]) for i in range(2)]
            H = [view(R3, 2 + KB * i, [F]) for i in range(NH_)]
            HT = [view(R3, 6 + 2 * i, [IC, P]) for i in range(2)]
            Z = [view(R3, 10 + i, [D]) for i in range(2)]
            G2 = [view(R3, a_, [D]) for a_ in (12, 13, 5)][0:NH_]
            gx_free, xs_free, ht_free, h_free = ([list(r3_free) for _ in range(3)] for _ in range(4))
            z_free = [list(r3_free) for _ in range(2)]
            st["gathered"] = 0

            def gather_to(n):
                while st["gathered"] < min(n, NT):
                    gather(st["gathered"])
                    st["gathered"] += 1

            def gather(g):
                j = g % 3
                st["gx", g] = pool.dma([*stored, tok_done, *gx_free[j]], lambda e: e.indirect_dma_start(
                    GX[j][:, :], None, xn_dram[layer], bass.IndirectOffsetOnAxis(tok_of[:, g:g + 1], 0)),
                    gx_sem[layer][j])

            def turn_x(g):
                j, bk = g % 2, 4
                for dc in range(DC):
                    tr = pe.add([st["gx", g], *free[bk]], lambda e, dc=dc: e.transpose(
                        bank[bk][:, dc * P:(dc + 1) * P], GX[g % 3][:, dc * P:(dc + 1) * P], ident), mark=dc == DC - 1)
                gx_free[g % 3] = [tr]
                st["xs", g] = copy_on(act, [tr, *xs_free[j]], xsT[j],
                                      bank[bk][:, 0:D].rearrange("p (a b) -> p a b", a=DC))
                free[bk] = [st["xs", g]]
                gather_to(g + 4)

            def up_banks(g):
                if layer == 0:
                    k = 2 * (g % 2)
                    return [k, k + 1], bank[k], bank[k + 1]
                return [g % 4], bank[g % 4][:, 0:F], bank[g % 4][:, F:2 * F]

            def up(g):
                j, (bks, gate, _) = g % 2, up_banks(g)
                cell = {}

                def one(e, n, dc):
                    if not cell:
                        cell["v"] = e.value_load(exp_of[0:1, g:g + 1], min_val=0, max_val=NE - 1)
                    return e.matmul(bank[bks[n]], xsT[j][:, dc, :],
                                    W1[:, dc, bass.ds(cell["v"] * (2 * F) + n * 512, 512)],
                                    start=(dc == 0), stop=(dc == DC - 1))

                ms = []
                for n in range(len(bks)):
                    for dc in range(DC):
                        mm = pe.add([st["xs", g], ex_done, *w1_ready, *free[bks[n]]],
                                    lambda e, n=n, dc=dc: one(e, n, dc), mark=dc == DC - 1)
                    ms.append(mm)
                xs_free[j] = [mm]
                st["up", g] = ms
                if layer == 1:
                    u = G2[g % NH_]
                    a = act.add([ms[0], *h_free[g % NH_]], lambda e: e.activation(u, gate, ACT.Square))
                    a = dve.add([a], lambda e: e.tensor_scalar(
                        u, u, GELU_C * 0.044715, GELU_C, ALU.mult, ALU.add))
                    st["inner", g] = dve.add([a], lambda e: e.tensor_tensor(u, gate, u, ALU.mult))

            def activate(g):
                bks, gate, upv = up_banks(g)
                ms, h = st["up", g], H[g % NH_]
                if layer == 0:
                    a = act.add([ms[0], *h_free[g % NH_]], lambda e: e.activation(h, gate, ACT.Tanh, scale=0.5))
                else:
                    u = G2[g % NH_]
                    a = act.add([st["inner", g], *h_free[g % NH_]], lambda e: e.activation(h, u, ACT.Tanh))
                a = dve.add([a], lambda e: e.scalar_tensor_tensor(h, h, 1.0, gate, ALU.add, ALU.mult))
                a = dve.add([a, ms[-1]], lambda e: e.scalar_tensor_tensor(h, h, 0.5, upv, ALU.mult, ALU.mult))
                st["h", g] = a
                for b in bks:
                    free[b] = [a]

            def turn_h(g):
                j, bk, h = g % 2, 5 + g % 2, H[g % NH_]
                for ic in range(IC):
                    tr = pe.add([st["h", g], *free[bk]], lambda e, ic=ic: e.transpose(
                        bank[bk][:, ic * P:(ic + 1) * P], h[:, ic * P:(ic + 1) * P], ident), mark=ic == IC - 1)
                h_free[g % NH_] = [tr]
                st["ht", g] = copy_on(act, [tr, *ht_free[j]], HT[j],
                                      bank[bk][:, 0:F].rearrange("p (a b) -> p a b", a=IC))
                free[bk] = [st["ht", g]]

            def down(g):
                j, bk = g % 2, 7
                cell = {}

                def one(e, ic):
                    if "v" not in cell:
                        cell["v"] = e.value_load(exp_of[0:1, g:g + 1], min_val=0, max_val=NE - 1)
                    return e.matmul(bank[bk][:, 0:D], HT[j][:, ic, :], W2[:, ic, bass.ds(cell["v"] * D, D)],
                                    start=(ic == 0), stop=(ic == IC - 1))

                for ic in range(IC):
                    mm = pe.add([st["ht", g], *w2_ready, *free[bk]], lambda e, ic=ic: one(e, ic), mark=ic == IC - 1)
                ht_free[j] = [mm]
                zc = copy_on(dve, [mm, *z_free[j]], Z[j], bank[bk][:, 0:D])
                free[bk] = [zc]
                z_free[j] = [sp.dma([zc], lambda e: e.dma_start(ys_dram[layer][g * P:(g + 1) * P, :], Z[j]),
                                    z_sem[layer][j])]
                st["down"] = mm

            gather_to(3)
            for g in range(AH):
                turn_x(g)
                up(g)
                if layer == 0 or g:
                    activate(g if layer == 0 else g - 1)
            turn_x(AH)
            for g in range(NT):
                if g + AH < NT:
                    up(g + AH)
                if g + 1 < NT:
                    activate(g + 1)
                turn_h(g)
                if g + AH + 1 < NT:
                    turn_x(g + AH + 1)
                if g >= 1:
                    down(g - 1)
                if g == 4:
                    during()
            down(NT - 1)
            return xs_free[(NT - 1) % 2][0], st["down"], [z_sem[layer][i].token() for i in range(2)]

        YG = view(R2, 0, [TOPK * TT, D])
        yg_sem = [[counter(f"yg{l}_{c}") for c in range(TOPK * TT)] for l in range(2)]

        def combine(layer, z_tokens, slot_done, w_done, r2_free, finish, apply=lambda i: None):
            toks = {}

            def gather(i):
                for k in range(TOPK):
                    c = k * TT + i
                    toks[i, k] = pool.dma([*z_tokens, slot_done, *r2_free], lambda e, c=c: e.indirect_dma_start(
                        YG[:, c, :], None, ys_dram[layer], bass.IndirectOffsetOnAxis(slot_of[:, c:c + 1], 0)),
                        yg_sem[layer][c])

            for i in range(3):
                gather(i)
            for i in range(TT):
                tk = w_done
                for k in range(TOPK):
                    c = k * TT + i
                    tk = dve.add([toks[i, k], tk], lambda e, c=c, k=k, i=i: e.scalar_tensor_tensor(
                        X[:, i, :], YG[:, c, :], wts[:, k, i:i + 1], X[:, i, :], ALU.mult, ALU.add))
                finish(i, tk)
                if i + 3 < TT:
                    gather(i + 3)
                if i:
                    apply(i - 1)
            apply(TT - 1)

        store_sem = [[counter(f"store{l}_{i}") for i in range(TT)] for l in range(2)]

        def tile_steps(layer, rt, xn_free, xnT_free):
            stored, stats, normed = [], {}, {}

            def finish(i, x_ready):
                stats[i] = norm_stats(i, [x_ready])

            def apply(i):
                normed[i] = norm_apply(i, stats[i], xn_free)
                stored.append(sp.dma([normed[i]], lambda e: e.dma_start(
                    xn_dram[layer][i * P:(i + 1) * P, :], XN[:, i, :]), store_sem[layer][i]))

            def route(i):
                done = transpose_xn(i, xnT, 3 if i % 2 else 5, normed[i], act, xnT_free)
                route_tile(layer, i, normed[i], done, rt)

            return stored, finish, apply, route

        rt0 = {"lg_free": [], "junk_free": []}
        w2 = view(R2, 0, [F0 // P, NE, D])
        ld_w2 = []

        def load_w2(i):
            if i in (3, 7):
                n = i // 4
                ld_w2.append(load(f"ld_w2_{n}", w2[:, 2 * n:2 * n + 2, :, :], t["w2"][:, 2 * n:2 * n + 2, :, :],
                                  [at0.q_done[i]]))

        stored0, *steps0 = tile_steps(0, rt0, [], [q0_last_mm])
        at0.run(b_ready, *steps0, each=load_w2)
        tok_done, ex_done, slot_done, w_done = route(0, rt0["sorted"])
        w1f = view(R1, 0, [DC, NE * 2 * F0])
        w2f = view(R2, 0, [F0 // P, NE * D])

        r4_free = [rt0["sorted"], q0_last_mm]
        wq1, kcq1 = view(R4, 0, [NH, D]), view(R4, 16, [NH, QW])
        ld_raw1 = []

        def load_raw1():
            ld_raw1.append(load("ld_wq1", wq1, t["wq1"], r4_free))
            ld_raw1.append(load("ld_kcq1", kcq1, t["kcq1"], r4_free))

        up_done, down_done, z_tok = experts(0, w1f, w2f, F0, ld_w1, ld_w2, stored0, tok_done, ex_done,
                                            [at0.b_done, rt0["sorted"]], load_raw1)
        rt_free["exp"] = [down_done]

        CM = view(R1, 0, [DC, 2, NH * HQ])
        TTm = view(R1, 24, [NP, 2, 2, P])
        qr1, kr1 = view(R2, 16, [2, 8 * HQ]), view(R2, 22, [8, C])
        ckv1, wo1 = view(R1, 40, [NH, C]), view(R1, 44, [NH, D])
        ld_qr1 = load("ld_qr1", qr1, t["qr1"].rearrange("p a b c -> p a (b c)"), [down_done])
        ld_kr1 = load("ld_kr1", kr1, t["kr1"], [down_done])
        ld_ckv1 = load("ld_ckv1", ckv1, t["ckv1"], [up_done])
        ld_wo1 = load("ld_wo1", wo1, t["wo1"], [up_done])

        def expand_matrices():
            toks = []
            i = 0
            for hp in range(NP):
                for dc in range(DC):
                    bk = i % 4
                    for h2 in range(2):
                        h = 2 * hp + h2
                        mm = pe.add([*ld_raw1, *free[bk]], lambda e, bk=bk, h=h, h2=h2, dc=dc: e.matmul(
                            bank[bk][:, h2 * QW:(h2 + 1) * QW], wq1[:, h, dc * P:(dc + 1) * P], kcq1[:, h, :],
                            start=True, stop=True), mark=h2 == 1)
                    for c in range(2):
                        src = bank[bk][:, 0:2 * QW].rearrange("p (h c q) -> p h c q", h=2, c=2)[:, :, c, :]
                        dst = CM[:, dc, c, 2 * hp * HQ:(2 * hp + 2) * HQ].rearrange("p (h q) -> p h q", h=2)
                        tk = copy_on(act, [mm, up_done], dst, src)
                    free[bk] = [tk]
                    toks.append(tk)
                    i += 1
            return toks

        def latent_matrices():
            toks = []
            for p in range(NP):
                bk = 4 + p % 4
                hh, p4 = p // 4, p % 4
                rows = slice(64 * hh, 64 * hh + 64)
                for j in range(2):
                    blk = 3 * (p4 // 2) + p4 % 2 + j
                    for c in range(2):
                        mm = pe.add([ld_qr1, ld_kr1, *free[bk]], lambda e, bk=bk, j=j, c=c, blk=blk, rows=rows, p4=p4:
                                    e.matmul(bank[bk][:, (2 * j + c) * P:(2 * j + c + 1) * P],
                                             qr1[rows, c, blk * P:(blk + 1) * P],
                                             kr1[rows, 2 * p4:2 * p4 + 2, :].rearrange("p a b -> p (a b)"),
                                             start=True, stop=True), mark=(j == 1 and c == 1))
                for j in range(2):
                    tk = dve.add([mm, ld_masks], lambda e, bk=bk, j=j, p=p: e.tensor_tensor(
                        TTm[:, p, j, :, :], bank[bk][:, 2 * j * P:(2 * j + 2) * P].rearrange("p (a b) -> p a b", a=2),
                        bc(masks[:, 2 * (p % 2) + j, :], 2), ALU.mult))
                free[bk] = [tk]
                toks.append(tk)
            return toks

        xnT1_ready, stats1 = {}, {}

        def norm1_finish(i, x_ready):
            stats1[i] = norm_stats(i, [x_ready])

        def norm1_apply(i):
            normed1[i] = norm_apply(i, stats1[i], stored0)

        normed1 = {}
        cm_ready = expand_matrices()
        combine(0, z_tok, slot_done, w_done, [down_done], norm1_finish, norm1_apply)
        tt_ready = latent_matrices()
        b1_ready, raw1_done = output_matrices(ckv1, wo1, [ld_ckv1, ld_wo1], [at0.b_done])
        for i in range(TT):
            xnT1_ready[i] = transpose_xn(i, xnT, 6 + i % 2, normed1[i], act, [cm_ready[-1]])

        RO = [view(R1, 40 + 12 * i, [3, 2, 512]) for i in range(2)]
        PR = [view(R3, 8 + 4 * i, [2, 512]) for i in range(2)]
        pr_free = [[*b1_ready, z_tok[0], z_tok[1]]] * 2
        ro_free = [[raw1_done, *tt_ready]] * 2
        q1_ready = {}
        n = 0
        w_last_q = []

        def roped_block(gi, g, hf, j):
            blk, k, ps = 3 * g + j, roped_block.n % 2, roped_block.n % 2
            roped_block.n += 1
            bks = (2 * k, 2 * k + 1)
            mms = []
            for c in range(2):
                for dc in range(DC):
                    mm = pe.add([*cm_ready, *[xnT1_ready[i] for i in range(4 * hf + 4)], *free[bks[c]]],
                                lambda e, c=c, dc=dc: e.matmul(
                                    bank[bks[c]], CM[:, dc, c, blk * P:(blk + 1) * P],
                                    xnT[:, dc, hf * 512:(hf + 1) * 512], start=(dc == 0), stop=(dc == DC - 1)),
                                mark=dc == DC - 1)
                mms.append(mm)
            pr, ro = PR[ps], RO[gi % 2]
            tab = [bc(ropeq[:, j, v, :], 8) for v in range(4)]

            def v3(ap):
                return ap.rearrange("p (a b) -> p a b", b=S)

            for src, v, dst in ((0, 0, ro[:, j, 0, :]), (0, 3, pr[:, 1, :]), (1, 1, pr[:, 0, :]), (1, 2, ro[:, j, 1, :])):
                tk = dve.add([mms[src], ld_ropeq, *pr_free[ps], *ro_free[gi % 2]], lambda e, src=src, v=v, dst=dst:
                             e.tensor_tensor(v3(dst), v3(bank[bks[src]]), tab[v], ALU.mult))
                if v in (3, 2):
                    free[bks[src]] = [tk]
            for c in range(2):
                r = pool.add([tk], lambda e, c=c: e.tensor_tensor(
                    ro[:, j, c, :], ro[:, j, c, :], pr[:, c, :], ALU.add))
            pr_free[ps] = [r]
            return r

        roped_block.n = 0
        pr_free = [list(pr_free[0]), list(pr_free[1])]
        ro_free = [list(ro_free[0]), list(ro_free[1])]

        def latent_query(gi, g, hf, r):
            for p2 in range(2):
                p, bk = 2 * g + p2, 4 + (2 * gi + p2) % 4
                m = 0
                for j in range(2):
                    for c in range(2):
                        mm = pe.add([r, *tt_ready, *free[bk]], lambda e, j=j, c=c, m=m, p=p, p2=p2, bk=bk: e.matmul(
                            bank[bk], TTm[:, p, j, c, :], RO[gi % 2][:, p2 + j, c, :],
                            start=(m == 0), stop=(m == 3)), mark=m == 3)
                        m += 1
                tk = copy_on(act, [mm, x_done[-1]], Q[:, hf, p, :], bank[bk])
                free[bk] = [tk]
                q1_ready[p, hf] = tk
            ro_free[gi % 2] = [mm]

        x_done = [(dve.sem, dve.count)]
        at1 = Attention(lambda i: [q1_ready[p, i // 4] for p in range(NP)], [(pe.sem, pe.count), (dve.sem, dve.count)])
        todo = None
        gi = 0
        for hf in range(2):
            for g in range(4):
                for j in range(3):
                    r = roped_block(gi, g, hf, j)
                    if j == 1 and todo:
                        latent_query(*todo)
                        todo = None
                        if gi == 4:
                            at1.scores(0)
                            at1.exponential(0)
                        if gi == 5:
                            at1.scores(1)
                            at1.exponential(1)
                    if j == 2 and gi in (4, 5):
                        at1.normalise(gi - 4)
                todo = (gi, g, hf, r)
                gi += 1
        latent_query(*todo)

        rope_done = (pe.sem, pe.count)
        g1 = view(R1, 0, [DC, NE * 2 * F1])
        l1 = view(R1, 32, [F1 // P, NE * D])
        ld_g1 = [load("ld_g1", g1, t["g1"], [rope_done])]
        ld_l1 = [load("ld_l1", l1, t["l1"], [rope_done])]

        rt1 = {"lg_free": [ex_done], "junk_free": []}
        at1.et_free = [[(pool.sem, pool.count)]] * 2
        at1.et_free = [list(x_) for x_ in at1.et_free]
        stored1, *steps1 = tile_steps(1, rt1, [], [rope_done])
        at1.run(b1_ready, *steps1)
        tok1, ex1, slot1, w1_ = route(1, rt1["sorted"])
        up1, down1, z1 = experts(1, g1, l1, F1, ld_g1, ld_l1, stored1, tok1, ex1,
                                 [at1.b_done, rt1["sorted"], (act.sem, act.count)])
        out_sem = counter("out")

        def write_out(i, x_ready):
            sp.dma([x_ready], lambda e: e.dma_start(out[i * P:(i + 1) * P, :], X[:, i, :]), out_sem)

        combine(1, z1, slot1, w1_, [at1.q_done[TT - 1]], write_out)

        block = ctx.enter_context(nc.Block())

        @block.sync
        def _(e):
            sp.play(e)
            e.wait_ge(out_sem.sem, out_sem.count)

        @block.scalar
        def _(e):
            act.play(e)

        @block.vector
        def _(e):
            dve.play(e)

        @block.gpsimd
        def _(e):
            pool.play(e)

        @block.tensor
        def _(e):
            pe.play(e)


def tables():
    f = np.float32
    k, m = np.arange(P)[:, None], np.arange(P)[None, :]
    consts = np.stack([(k == m), (k < m), np.ones((P, P))], 1).astype(f)

    def rope(n, dim):
        inv = f(1.0) / np.power(f(10000.0), np.arange(0, dim, 2, dtype=f) / f(dim)).astype(f)
        fr = np.arange(n, dtype=f)[:, None] * inv[None, :]
        return np.repeat(np.sin(fr), 2, -1).astype(f), np.repeat(np.cos(fr), 2, -1).astype(f)

    sin, cos = rope(S, C)
    sign = np.where(np.arange(C) < C // 2, f(-1), f(1))
    ropek = np.concatenate([np.stack([cos, sin * sign], 1)] * 2, 0)
    sin, cos = rope(S, QW)
    ropeq = np.zeros((P, 3, 4, S), f)
    masks = np.zeros((P, 4, P), f)
    for j in range(3):
        row = P * j + np.arange(P)
        q = row % HQ
        ropeq[:, j, 0], ropeq[:, j, 1] = cos[:, q].T, -sin[:, q].T
        ropeq[:, j, 2], ropeq[:, j, 3] = cos[:, q + HQ].T, sin[:, q + HQ].T
        for odd in range(2):
            if odd <= j <= odd + 1:
                head = row // HQ - 2 * odd
                masks[:, 2 * odd + j - odd] = head[:, None] == (np.arange(P) // C)[None, :]
    small = np.zeros((P, 512), f)
    small[:, 0:8] = np.arange(8)
    small[:, 8:136] = np.arange(P)
    small[:, 136:152] = np.tile(np.arange(TT), TOPK)
    small[:, 152:216] = (np.arange(8)[None, :] < np.arange(8)[:, None]).reshape(-1)
    small[:, 216:216 + NT] = np.arange(NT)
    small[:, 248] = np.arange(P)
    return {"consts": consts, "ropek": ropek, "ropeq": ropeq, "masks": masks, "small": small}


def lay_out(i):
    a = {"x": i["x"].reshape(TT, P, D).transpose(1, 0, 2), "ctx": i["ctx_512"].transpose(1, 0, 2)}
    for l in range(2):
        def w(n):
            return i[f"L{l}_xattn_{n}"]
        a[f"qr{l}"] = w("W_qr").reshape(2, 8, 2, HQ, 64).transpose(0, 4, 2, 1, 3).reshape(P, 2, 8, HQ)
        a[f"kr{l}"] = w("W_kr").reshape(2, 8, C, 64).transpose(0, 3, 1, 2).reshape(P, 8, C)
        a[f"wq{l}"] = w("Wq").reshape(NH, HK, D).transpose(1, 0, 2)
        a[f"ckv{l}"] = w("w_kc_kv").transpose(1, 0, 2)
        a[f"wo{l}"] = w("Wo").reshape(D, NH, HK).transpose(2, 1, 0)
    a["kcq0"] = i["L0_xattn_w_kc_q"].reshape(NH, HK, 2, HQ).transpose(3, 2, 0, 1)
    a["kcq1"] = i["L1_xattn_w_kc_q"].transpose(1, 0, 2)
    a["w1"] = i["L0_ffn_w1"].reshape(NE, 2 * F0, DC, P).transpose(3, 2, 0, 1)
    a["w2"] = i["L0_ffn_w2"].reshape(NE, D, F0 // P, P).transpose(3, 2, 0, 1)
    a["g1"] = i["L1_ffn_gating_einsum"].reshape(NE, 2 * F1, DC, P).transpose(3, 2, 0, 1).reshape(P, DC, NE * 2 * F1)
    a["l1"] = i["L1_ffn_linear"].reshape(NE, F1 // P, P, D).transpose(2, 1, 0, 3).reshape(P, F1 // P, NE * D)
    a["rout"] = np.stack([i["L0_ffn_router_w"].reshape(NE, DC, P).transpose(2, 1, 0),
                          i["L1_ffn_router_logits"].reshape(DC, P, NE).transpose(1, 0, 2)], 1)
    a["rscale"] = i["L1_ffn_router_scale"].reshape(DC, P).T
    a["pes"] = np.broadcast_to(i["L1_ffn_per_expert_scale"], (P, NE))
    return a


def kernel(**inputs):
    import concourse.bacc as _bacc
    from concourse.bass_utils import run_bass_kernel_spmd as _run

    nc = _bacc.Bacc("TRN2", target_bir_lowering=False, num_devices=1)
    arrays, aps = {}, {}
    for name, a in {**lay_out({k: np.asarray(v) for k, v in inputs.items()}), **tables()}.items():
        arrays[f"in_{name}"] = np.ascontiguousarray(a)
        aps[name] = nc.dram_tensor(f"in_{name}", a.shape, mybir.dt.from_np(a.dtype), kind="ExternalInput").ap()
    out = nc.dram_tensor("out", [TOK, D], F32, kind="ExternalOutput").ap()
    build(nc, aps, out)
    r = _run(nc, [arrays], core_ids=[0])
    return r.results[0]["out"].reshape(NB, S, D)
```

```python
from contextlib import ExitStack

import numpy as np

import concourse.bass as bass
from concourse import mybir
from concourse.alu_op_type import AluOpType as ALU

F32 = mybir.dt.float32
F32R = mybir.dt.float32r
BF16 = mybir.dt.bfloat16
I32 = mybir.dt.int32
U32 = mybir.dt.uint32
ACT = mybir.ActivationFunctionType
AX = mybir.AxisListType.X

P = 128
NB, S = 16, 64
TOK = NB * S
TT = TOK // P
D = 256
DC = D // P
NH, HK = 16, 128
NP = NH // 2
C = 64
QW, HQ = 192, 96
NBLK = NH * HQ // P
NE, TOPK = 8, 2
NT = TOK * TOPK // P + NE - 1
F0, F1 = 512, 256
EPS = 1e-5
GELU_C = float(np.sqrt(2.0 / np.pi))


class Queue:

    def __init__(self, sem):
        self.sem, self.count, self.items = sem, 0, []

    def add(self, waits, fn, mark=True):
        self.count += mark
        self.items.append((waits, fn, self.sem if mark else None, 1))
        return (self.sem, self.count)

    def dma(self, waits, fn, sem):
        sem.count += 16
        self.items.append((waits, fn, sem.sem, 16))
        return (sem.sem, sem.count)

    def play(self, eng):
        reached = {}
        for waits, fn, sem, by in self.items:
            for s, v in waits:
                if reached.get(id(s), 0) < v:
                    eng.wait_ge(s, v)
                    reached[id(s)] = v
            ins = fn(eng)
            if sem is not None:
                ins.then_inc(sem, by)


class Counter:
    def __init__(self, sem):
        self.sem, self.count = sem, 0

    def token(self):
        return (self.sem, self.count)


def copy_on(queue, waits, out, in_):
    return queue.add(waits, lambda e: (e.copy if hasattr(e, "copy") else e.tensor_copy)(out, in_))


def build(nc, t, out):
    with ExitStack() as ctx:
        def sb(name, shape, dt=F32):
            return ctx.enter_context(nc.sbuf_tensor(name, shape, dt))

        def sem(name):
            return ctx.enter_context(nc.semaphore(name))

        def counter(name):
            return Counter(sem(name))

        sp, act, dve, pool, pe = (Queue(sem(n)) for n in ("s_sp", "s_act", "s_dve", "s_pool", "s_pe"))

        xn_dram = [nc.dram_tensor(f"xn_dram{i}", [TOK, D], F32).ap() for i in range(2)]
        ys_dram = [nc.dram_tensor(f"ys_dram{i}", [NT * P, D], F32).ap() for i in range(2)]

        X = sb("X", [P, TT, D])
        XN = sb("XN", [P, TT, D])
        VB = sb("VB", [P, NB, P])
        KT = sb("KT", [P, NB, P])
        B = sb("B", [P, NP, D])
        consts = sb("consts", [P, 3, P])
        ident, before, ones = (consts[:, i, :] for i in range(3))
        ropeq = sb("ropeq", [P, 6, S])
        small = sb("small", [P, 512])

        def under(*names_kb):
            with ExitStack() as now:
                return [now.enter_context(nc.sbuf_tensor(n, [P, kb * 256], F32R)) for n, kb in names_kb]

        AL_, = under(("A_lo", 8))
        CMH_, CML_ = under(("CM_hi", 24), ("CM_lo", 24))
        R1 = sb("R1", [P, 64 * 256])
        R2 = sb("R2", [P, 32 * 256])
        R3 = sb("R3", [P, 25 * 256])
        XTH_, XTL_, AH_ = under(("xnT_hi", 8), ("xnT_lo", 8), ("A_hi", 8))
        R4 = sb("R4", [P, 28 * 256])
        stat = sb("stat", [P, 64])
        before16, ones16 = sb("before16", [P, P], BF16), sb("ones16", [P, P], BF16)
        lnst = sb("lnst", [P, TT, 10])
        PSD = [ctx.enter_context(nc.psum_tensor(f"PSD{i}", [P, 2, 512], F32)) for i in range(4)]
        bank = [PSD[i // 2][:, i % 2, :] for i in range(8)]
        free = [[] for _ in range(8)]

        def view(region, at_kb, shape, parts=P, p0=0):
            n = int(np.prod(shape))
            v = region[p0:p0 + parts, at_kb * 256:at_kb * 256 + n]
            if len(shape) == 1:
                return v
            names = "abcd"[:len(shape)]
            return v.rearrange(f"p ({' '.join(names)}) -> p {' '.join(names)}",
                               **{k: s for k, s in zip(names[1:], shape[1:])})

        def load(name, dst, src, waits=()):
            return sp.dma(list(waits), lambda e: e.dma_start(dst, src), counter(name))

        qr0, kr0 = view(R4, 16, [NP, QW]), view(R4, 22, [NP, P])
        kcq0 = view(R1, 8, [2, NH, HK], parts=HQ)
        wq0, ckv0, wo0 = view(R1, 24, [NH, D]), view(R1, 40, [NH, C]), view(R1, 44, [NH, D])
        ctx_in = view(R3, 0, [NB, C])
        ctx_rope = view(R3, 4, [2, C])
        ctx_cos = view(R3, 5, [NB, C])
        ctx_sin = view(R3, 9, [NB, C])
        rout = sb("rout", [P, 2, DC, NE])
        rscale = sb("rscale", [P, DC])
        pes = sb("pes", [P, NE])
        ld_x, ld_kcq0, ld_wq0 = [], [], []
        ld_qr0 = load("ld_qr0", qr0, t["qr0"])
        ld_kr0 = load("ld_kr0", kr0, t["kr0"])
        for i in range(2):
            hs = slice(8 * i, 8 * i + 8)
            ld_x.append(load(f"ld_x{i}", X[:, 4 * i:4 * i + 4, :], t["x"][:, 4 * i:4 * i + 4, :]))
            if i == 0:
                ld_c = load("ld_consts", consts[:, :, :], t["consts"])
            ld_kcq0.append(load(f"ld_kcq0_{i}", kcq0[:, :, hs, :], t["kcq0"][:, :, hs, :]))
            ld_wq0.append(load(f"ld_wq0_{i}", wq0[:, hs, :], t["wq0"][:, hs, :]))
        ld_ctx = sp.dma([], lambda e: e.dma_start(ctx_in[0:64], t["ctx"]), counter("ld_ctx0"))
        ld_ctx2 = sp.dma([], lambda e: e.dma_start(ctx_in[64:128], t["ctx"]), counter("ld_ctx1"))
        ld_rk = load("ld_ropek", ctx_rope, t["ropek"])
        ld_ckv0 = load("ld_ckv0", ckv0, t["ckv0"])
        ld_wo0 = load("ld_wo0", wo0, t["wo0"])
        ld_small = load("ld_small", small[:, :], t["small"])
        ld_rout = load("ld_rout", rout[:, :, :, :], t["rout"])
        ld_rs = load("ld_rscale", rscale[:, :], t["rscale"])
        ld_pes = load("ld_pes", pes[:, :], t["pes"])
        ld_ropeq = load("ld_ropeq", ropeq[:, :, :], t["ropeq"])

        half_neg = stat[:, 0:1]
        z_half = pool.add([], lambda e: e.memset(half_neg, -0.5))

        def norm_stats(tile, waits):
            bn, mv, ve = lnst[:, tile, 0:6], lnst[:, tile, 6:8], lnst[:, tile, 8:9]
            a = dve.add(list(waits), lambda e: e.bn_stats(bn, X[:, tile, :]))
            a = dve.add([a], lambda e: e.bn_aggr(mv, bn))
            a = dve.add([a], lambda e: e.tensor_scalar(ve, mv[:, 1:2], EPS, None, ALU.add))
            return pool.add([a, z_half], lambda e: e.tensor_tensor(lnst[:, tile, 9:10], ve, half_neg, ALU.pow))

        def norm_apply(tile, stats, waits=()):
            return dve.add([stats, *waits], lambda e: e.tensor_scalar(
                XN[:, tile, :], X[:, tile, :], lnst[:, tile, 6:7], lnst[:, tile, 9:10], ALU.subtract, ALU.mult))

        def transpose_xn(tile, b, xn_ready):
            for dc in range(DC):
                tr = pe.add([xn_ready, ld_c, *free[b]], lambda e, dc=dc: e.transpose(
                    bank[b][:, dc * P:(dc + 1) * P], XN[:, tile, dc * P:(dc + 1) * P], ident), mark=dc == DC - 1)
            return tr, bank[b][:, 0:DC * P].rearrange("p (a b) -> p a b", a=DC)

        def split(ready, hi, lo, src, banks, waits=()):
            a = act.add([ready, *waits], lambda e: e.copy(hi, src))
            a = dve.add([a], lambda e: e.tensor_tensor(lo, src, hi.bitcast(F32), ALU.subtract))
            for b in banks:
                free[b] = [a]
            return a

        def product(out, wh, wl, xh, xl, waits, first, last):
            for i, (w_, x_) in enumerate(((wh, xh), (wh, xl), (wl, xh))):
                mm = pe.add(waits, lambda e, i=i, w_=w_, x_=x_: e.matmul(
                    out, w_, x_, start=first and i == 0, stop=last and i == 2), mark=last and i == 2)
            return mm

        def split_xn(tile, b, xn_ready, waits=()):
            tr, src = transpose_xn(tile, b, xn_ready)
            cols = slice(tile * P, (tile + 1) * P)
            return split(tr, XH[:, :, cols], XL[:, :, cols], src, [b], waits)

        H2 = C // 2

        def bc(ap, n):
            return ap.unsqueeze(1).to_broadcast([ap.shape[0], n, ap.shape[1]])

        zv = pool.add([], lambda e: e.memset(VB[:, :, :], 0.0))

        XH, XL = (v_[:, :].rearrange("p (a b) -> p a b", a=DC) for v_ in (XTH_, XTL_))
        xnT = view(R4, 0, [DC, TOK])
        T1 = view(R3, 13, [2, NH, C], parts=HQ)
        T2 = view(R3, 21, [NH, C])
        AH, AL = (v_[:, :].rearrange("p (a b) -> p a b", a=DC) for v_ in (AH_, AL_))
        t1_ready, t2_ready, a_ready, xnT_ready = {}, {}, {}, []

        def first_products(hh):
            for c in range(2):
                bk = 2 + 2 * hh + c
                for p4 in range(4):
                    p = 4 * hh + p4
                    mm = pe.add([ld_qr0, ld_kr0, *free[bk]], lambda e, bk=bk, c=c, p=p, p4=p4: e.matmul(
                        bank[bk][0:HQ, p4 * P:(p4 + 1) * P], qr0[:, p, c * HQ:(c + 1) * HQ], kr0[:, p, :],
                        start=True, stop=True), mark=p4 == 3)
                tk = copy_on(act, [mm], T1[:, c, 8 * hh:8 * hh + 8, :],
                             bank[bk][0:HQ, :].rearrange("p (a b) -> p a b", a=8))
                free[bk] = [tk]
                t1_ready[hh, c] = tk

        def second_products(hh):
            bk = hh
            for h8 in range(8):
                h = 8 * hh + h8
                for c in range(2):
                    mm = pe.add([ld_kcq0[hh], t1_ready[hh, 0], t1_ready[hh, 1], *free[bk]],
                                lambda e, bk=bk, h=h, h8=h8, c=c: e.matmul(
                                    bank[bk][:, h8 * C:(h8 + 1) * C], kcq0[:, c, h, :], T1[:, c, h, :],
                                    start=(c == 0), stop=(c == 1)), mark=(h8 == 7 and c == 1))
            tk = copy_on(act, [mm], T2[:, 8 * hh:8 * hh + 8, :], bank[bk].rearrange("p (a b) -> p a b", a=8))
            free[bk] = [tk]
            t2_ready[hh] = tk

        def third_products(hh):
            for dc in range(DC):
                bk = 2 + 2 * dc + hh
                for h8 in range(8):
                    h = 8 * hh + h8
                    mm = pe.add([ld_wq0[hh], t2_ready[hh], *free[bk]], lambda e, bk=bk, h=h, h8=h8, dc=dc: e.matmul(
                        bank[bk][:, h8 * C:(h8 + 1) * C], wq0[:, h, dc * P:(dc + 1) * P], T2[:, h, :],
                        start=True, stop=True), mark=h8 == 7)
                cols = slice(512 * hh, 512 * hh + 512)
                a_ready[hh, dc] = split(mm, AH[:, dc, cols], AL[:, dc, cols], bank[bk], [bk])

        def first_norm(tiles):
            stats = [norm_stats(i, [ld_x[i // 4]]) for i in tiles]
            normed = [norm_apply(i, s_) for i, s_ in zip(tiles, stats)]
            for i, xn in zip(tiles, normed):
                xnT_ready.append(split_xn(i, 6 + i % 2, xn))

        first_products(0)
        first_products(1)
        first_norm(range(4))
        second_products(0)
        third_products(0)
        second_products(1)
        first_norm(range(4, 8))

        a = dve.add([ld_ctx, ld_ctx2, ld_rk], lambda e: e.tensor_tensor(
            ctx_cos, ctx_in, bc(ctx_rope[:, 0, :], NB), ALU.mult))
        b_ = dve.add([], lambda e: e.tensor_tensor(ctx_sin[:, :, 0:H2], ctx_in[:, :, H2:C],
                                                   bc(ctx_rope[:, 1, 0:H2], NB), ALU.mult))
        b_ = dve.add([], lambda e: e.tensor_tensor(ctx_sin[:, :, H2:C], ctx_in[:, :, 0:H2],
                                                   bc(ctx_rope[:, 1, H2:C], NB), ALU.mult))
        for par in range(2):
            h = slice(64 * par, 64 * par + 64)
            vb_ready = dve.add([b_, zv], lambda e, h=h: e.tensor_tensor(
                VB[h, :, h], ctx_cos[h], ctx_sin[h], ALU.add))
        kt_ready = []

        def turn_context():
            for i in range(4):
                bk = 6 + i % 2
                for j in range(4):
                    tr = pe.add([vb_ready, *free[bk]], lambda e, bk=bk, i=i, j=j: e.transpose(
                        bank[bk][:, j * P:(j + 1) * P], VB[:, 4 * i + j, :], ident), mark=j == 3)
                tk = copy_on(act if i % 2 else dve, [tr], KT[:, 4 * i:4 * i + 4, :],
                             bank[bk].rearrange("p (a b) -> p a b", a=4))
                free[bk] = [tk]
                kt_ready.append(tk)

        def output_matrices(ckv, wo, waits, b_waits, engines):
            toks = []
            for i in range(4):
                bk = 2 + i
                for p2 in range(2):
                    for par in range(2):
                        h = 4 * i + 2 * p2 + par
                        mm = pe.add([*waits, *free[bk]], lambda e, bk=bk, h=h, p2=p2, par=par: e.matmul(
                            bank[bk][64 * par:64 * par + 64, p2 * D:(p2 + 1) * D], ckv[:, h, :], wo[:, h, :],
                            start=True, stop=True), mark=(p2 == 1 and par == 1))
                tk = copy_on(engines[i % 2], [mm, *b_waits], B[:, 2 * i:2 * i + 2, :],
                             bank[bk].rearrange("p (a b) -> p a b", a=2))
                free[bk] = [tk]
                toks.append(tk)
            return toks, mm

        Q = view(R2, 0, [2, NP, TOK // 2])
        q_ready = {}
        turn_q = [0]

        def latent_queries0(hf, hh):
            toks = []
            for p in range(4 * hh, 4 * hh + 4):
                bk = turn_q[0] % 4
                turn_q[0] += 1
                rows, cols = slice(p * P, (p + 1) * P), slice(hf * 512, (hf + 1) * 512)
                for dc in range(DC):
                    mm = product(bank[bk], AH[:, dc, rows], AL[:, dc, rows], XH[:, dc, cols], XL[:, dc, cols],
                                 [a_ready[hh, 0], a_ready[hh, 1], *xnT_ready[4 * hf:4 * hf + 4], *free[bk]],
                                 dc == 0, dc == DC - 1)
                toks.append(copy_on(act if p % 2 else dve, [mm], Q[:, hf, p, :], bank[bk]))
                free[bk] = [toks[-1]]
            q_ready[hf, hh] = toks

        latent_queries0(0, 0)
        third_products(1)
        latent_queries0(0, 1)
        turn_context()

        class Attention:

            def __init__(self, q_ready, r3_free):
                self.q_ready = q_ready
                self.E = [view(R3, 4 * i, [NH, S]) for i in range(2)]
                self.ET = [view(R3, 8 + 4 * i, [NP, P]) for i in range(2)]
                self.CT = [view(R3, 16 + 4 * i, [NP, P]) for i in range(2)]
                self.mx, self.sm, self.rs = ([sbm[:, 32 * k + 16 * i:32 * k + 16 * i + 16] for i in range(2)]
                                             for k in range(3))
                self.e_free = [list(r3_free), list(r3_free)]
                self.et_free = [list(r3_free), list(r3_free)]
                self.ct_free = [list(r3_free), list(r3_free)]
                self.e, self.sub, self.et, self.ct, self.q_done = {}, {}, {}, {}, {}

            def pair(self, k):
                return k, [*free[2 * k], *free[2 * k + 1]]

            def scores(self, i):
                k, k_free = self.pair(i if i < 2 else 2)
                for p in range(NP):
                    for b2 in range(2):
                        b = 2 * i + b2
                        mm = pe.add([*self.q_ready(i), *kt_ready, *k_free], lambda e, p=p, b=b, b2=b2: e.matmul(
                            bank[2 * k + p // 4][64 * b2:64 * b2 + 64, (p % 4) * P:(p % 4 + 1) * P],
                            Q[:, i // 4, p, (b % 8) * S:(b % 8 + 1) * S], KT[:, b, :], start=True, stop=True),
                            mark=(p == NP - 1 and b2 == 1))
                self.q_done[i] = mm
                E, mx = self.E[i % 2], self.mx[i % 2]
                ps = PSD[k][:, :, :].rearrange("p a (h l) -> p (a h) l", l=S)
                m = dve.add([mm, *self.e_free[i % 2]], lambda e: e.tensor_reduce(mx, ps, AX, ALU.max))
                self.sub[i] = dve.add([m], lambda e: e.tensor_tensor(
                    E, ps, mx.unsqueeze(2).to_broadcast([P, NH, S]), ALU.subtract))
                free[2 * k] = free[2 * k + 1] = [self.sub[i]]

            def exponential(self, i):
                E = self.E[i % 2]
                self.e[i] = act.add([self.sub[i]], lambda e: e.activation(E, E, ACT.Exp))

            def normalise(self, i):
                E, sm, rs = self.E[i % 2], self.sm[i % 2], self.rs[i % 2]
                s = dve.add([self.e[i]], lambda e: e.tensor_reduce(sm, E, AX, ALU.add))
                s = dve.add([s], lambda e: e.reciprocal(rs, sm))
                self.e[i] = pool.add([s], lambda e: e.tensor_tensor(
                    E, E, rs.unsqueeze(2).to_broadcast([P, NH, S]), ALU.mult))

            def turn_weights(self, i):
                (k, k_free), j = self.pair(1), i % 2
                for p in range(NP):
                    tr = pe.add([self.e[i], *k_free], lambda e, p=p: e.transpose(
                        bank[2 * k + p // 4][:, (p % 4) * P:(p % 4 + 1) * P],
                        self.E[j][:, 2 * p:2 * p + 2, :].rearrange("p a b -> p (a b)"), ident), mark=p == NP - 1)
                self.e_free[j] = [tr]
                self.et[i] = copy_on(act, [tr, *self.et_free[j]], self.ET[j],
                                     PSD[k][:, :, :].rearrange("p a (h l) -> p (a h) l", l=P))
                free[2 * k] = free[2 * k + 1] = [self.et[i]]

            def weighted_context(self, i):
                (k, k_free), j = self.pair(3), i % 2
                self.ct[i] = []
                for b2 in range(2):
                    mm = pe.add([self.et[i], *k_free], lambda e, b2=b2: e.matmul(
                        bank[2 * k + b2], VB[:, 2 * i + b2, :], self.ET[j][:, :, b2 * S:(b2 + 1) * S],
                        start=True, stop=True))
                    tk = copy_on(act if b2 else dve, [mm, *self.ct_free[j]], self.CT[j][:, :, b2 * S:(b2 + 1) * S],
                                 bank[2 * k + b2].rearrange("p (a b) -> p a b", b=S))
                    free[2 * k + b2] = [tk]
                    self.ct[i].append(tk)
                self.et_free[j] = [mm]

            def project(self, i, b_ready, finish):
                k, j = 0, i % 2
                for p in range(NP):
                    mm = pe.add([*self.ct[i], *b_ready, *free[2 * k]], lambda e, p=p: e.matmul(
                        bank[2 * k][:, 0:D], self.CT[j][:, p, :], B[:, p, :], start=(p == 0), stop=(p == NP - 1)),
                        mark=p == NP - 1)
                self.ct_free[j] = [mm]
                self.b_done = mm
                tk = dve.add([mm], lambda e: e.tensor_tensor(X[:, i, :], bank[2 * k][:, 0:D], X[:, i, :], ALU.add))
                free[2 * k] = [tk]
                finish(i, tk)

            def run(self, b_ready, finish, apply, turn, route, each=lambda i: None):
                for i in range(TT + 3):
                    if i < TT:
                        self.turn_weights(i)
                    if i + 2 < TT:
                        self.scores(i + 2)
                        self.exponential(i + 2)
                        each(i + 2)
                    if 0 <= i - 2 < TT:
                        apply(i - 2)
                    if 0 <= i - 3 < TT:
                        turn(i - 3)
                    if i < TT:
                        self.weighted_context(i)
                    if i + 2 < TT:
                        self.normalise(i + 2)
                    if 0 <= i - 1 < TT:
                        self.project(i - 1, b_ready, finish)
                    if 0 <= i - 3 < TT:
                        route(i - 3)

        sbm = sb("sbm", [P, 96])

        at0 = Attention(lambda i: [*q_ready[i // 4, 0], *q_ready[i // 4, 1]],
                        [a_ready[1, 0], a_ready[1, 1], vb_ready])
        at0.scores(0)
        at0.exponential(0)
        latent_queries0(1, 0)
        at0.normalise(0)
        latent_queries0(1, 1)
        q0_last_mm = (pe.sem, pe.count)
        at0.scores(1)
        at0.exponential(1)
        b_ready, raw0_done = output_matrices(ckv0, wo0, [ld_ckv0, ld_wo0], [], (act, dve))
        at0.normalise(1)

        w1 = view(R1, 0, [DC, NE, 2 * F0])
        ld_w1 = [load(f"ld_w1_{i}", w1[:, i, :, :], t["w1"][:, i, :, :], [raw0_done]) for i in range(DC)]

        io_e, io_r = small[:, 0:8], small[:, 8:136]
        tile_of = small[:, 136:152]
        tri_e = small[:, 152:216].rearrange("p (a b) -> p a b", a=NE)
        io_g, pid = small[:, 216:216 + NT], small[:, 248:249]
        dve.add([ld_c], lambda e: e.tensor_copy(before16[:, :], before))
        bf16_ready = dve.add([], lambda e: e.tensor_copy(ones16[:, :], ones))
        rout1_ready = [dve.add([ld_rs, ld_rout], lambda e, dc=dc: e.tensor_scalar(
            rout[:, 1, dc, :], rout[:, 1, dc, :], rscale[:, dc:dc + 1], None, ALU.mult)) for dc in range(DC)]

        LG = sb("LG", [P, TT, NE])
        VAL = sb("VAL", [P, TT, 8])
        IDX = sb("IDX", [P, TT, 8], U32)
        RT = view(R3, 14, [1024])
        RTI = sb("RTI", [P, 96], I32)
        OHR = R3[:, 18 * 256:22 * 256].bitcast(BF16).rearrange("p (a b) -> p a b", b=P)
        OHG = R3[:, 22 * 256:22 * 256 + 3 * TOPK * TT * NT // 2].bitcast(BF16).rearrange(
            "p (v a b) -> p v a b", v=3, b=NT)
        tok_of = sb("tok_of", [P, NT], I32)
        slot_of = sb("slot_of", [P, TOPK * TT], I32)
        exp_of = sb("exp_of", [P, NT], I32)
        wts = sb("wts", [P, TOPK, TT])
        rms = sb("rms", [P, 3, TT])

        def router_factor(i, xn_ready, rt):
            ms, me, mr = (rms[:, n, i:i + 1] for n in range(3))
            junk = view(R3, 24, [D])
            a = act.add([xn_ready, *rt["junk_free"]], lambda e: e.activation(
                junk, XN[:, i, :], ACT.Square, accum_out=ms))
            rt["junk_free"] = [a]
            a = dve.add([a], lambda e: e.tensor_scalar(me, ms, 1.0 / D, 1e-6, ALU.mult, ALU.add))
            return pool.add([a], lambda e: e.tensor_tensor(mr, me, half_neg, ALU.pow))

        def route_tile(layer, i, xnT_done, factor, rt):
            bk = 6
            for dc in range(DC):
                mm = pe.add([xnT_done, ld_rout, *rout1_ready, *free[bk]], lambda e, dc=dc: e.matmul(
                    bank[bk][:, 0:NE], rt_xnT[:, dc, i * P:(i + 1) * P], rout[:, layer, dc, :],
                    start=(dc == 0), stop=(dc == DC - 1)), mark=dc == DC - 1)
            if layer == 0:
                lg = dve.add([mm, *rt["lg_free"]], lambda e: e.tensor_copy(LG[:, i, :], bank[bk][:, 0:NE]))
            else:
                lg = dve.add([factor, mm, *rt["lg_free"]], lambda e: e.tensor_scalar(
                    LG[:, i, :], bank[bk][:, 0:NE], rms[:, 2, i:i + 1], float(D) ** -0.5, ALU.mult, ALU.mult))
            free[bk] = [lg]
            v = dve.add([lg], lambda e: e.max(VAL[:, i, :], LG[:, i, :]))
            rt["sorted"] = dve.add([v], lambda e: e.max_index(IDX[:, i, :], VAL[:, i, :], LG[:, i, :]))

        rt_xnT = xnT

        rt_extra = []

        def route(layer, srt, meanwhile=lambda: None):
            n = [0]

            def take(k):
                v = RT[:, n[0]:n[0] + k]
                n[0] += k
                return v

            KT_ = TOPK * TT
            ev, ssum, srec = take(64).rearrange("p (a b) -> p a b", a=TT), take(8), take(8)
            w = dve.add([srt], lambda e: e.tensor_tensor(
                ev, VAL[:, :, :], VAL[:, :, 0:1].to_broadcast([P, TT, 8]), ALU.subtract))
            w = act.add([w], lambda e: e.activation(ev, ev, ACT.Exp))
            idf = take(KT_).rearrange("p (a b) -> p a b", a=TOPK)
            oh = take(KT_ * NE)
            oh3 = oh.rearrange("p (a b) -> p a b", b=NE)
            m = take(32).bitcast(BF16)
            for k in range(TOPK):
                a = dve.add([], lambda e, k=k: e.tensor_copy(idf[:, k, :], IDX[:, :, k]))
            a = dve.add([a, ld_small], lambda e: e.tensor_tensor(
                oh3, bc(io_e, KT_), idf.rearrange("p a b -> p (a b)").unsqueeze(2).to_broadcast([P, KT_, NE]),
                ALU.is_equal))
            a = dve.add([a], lambda e: e.tensor_tensor(m, oh[:, 0:64], oh[:, 64:128], ALU.add))
            rank_bank = 0
            pe.add([a, bf16_ready, *free[rank_bank]], lambda e: e.matmul(bank[rank_bank][:, 0:64], before16[:, :], m, start=True, stop=False,
                                                      skip_group_check=True), mark=False)
            for i in range(TT):
                mm = pe.add([], lambda e, i=i: e.matmul(
                    bank[rank_bank][:, 8 * (i + 1):8 * (TT + 1)].rearrange("p (a b) -> p a b", b=NE), ones16[:, :],
                    bc(m[:, 8 * i:8 * i + 8], TT - i), start=False, stop=(i == TT - 1),
                    skip_group_check=True), mark=i == TT - 1)
            rank = take(72)
            r = dve.add([mm], lambda e: e.tensor_copy(rank, bank[rank_bank][:, 0:72]))
            free[rank_bank] = [r]
            rt_extra.append(meanwhile())
            cnt_i, nt_f, prod = RTI[:, 0:8], take(8), take(64).rearrange("p (a b) -> p a b", a=NE)
            first, last, base = take(8), take(8), take(64).rearrange("p (a b) -> p a b", a=TT)
            a = dve.add([r], lambda e: e.tensor_scalar(cnt_i, rank[:, 64:72], float(P - 1), None, ALU.add))
            a = dve.add([a], lambda e: e.tensor_scalar(cnt_i, cnt_i, 7, None, ALU.logical_shift_right))
            a = dve.add([a], lambda e: e.tensor_copy(nt_f, cnt_i))
            a = dve.add([a], lambda e: e.tensor_tensor(prod, tri_e, bc(nt_f, NE), ALU.mult))
            a = dve.add([a], lambda e: e.tensor_reduce(first, prod, AX, ALU.add))
            a = dve.add([a], lambda e: e.tensor_tensor(last, first, nt_f, ALU.add))
            a1 = dve.add([], lambda e: e.scalar_tensor_tensor(
                base, bc(first, TT), float(P), rank[:, 0:64].rearrange("p (a b) -> p a b", a=TT),
                ALU.mult, ALU.add))
            sel, slot_f = take(KT_ * NE), take(KT_)
            a1 = dve.add([a1], lambda e: e.tensor_tensor(
                sel.rearrange("p (k x) -> p k x", k=TOPK), oh.rearrange("p (k x) -> p k x", k=TOPK),
                bc(base.rearrange("p a b -> p (a b)"), TOPK), ALU.mult))
            a1 = dve.add([a1], lambda e: e.tensor_reduce(slot_f, sel.rearrange("p (a b) -> p a b", b=NE), AX, ALU.add))
            slot_done = dve.add([a1], lambda e: e.tensor_copy(slot_of[:, :], slot_f))
            g_i, r_i, g_f, r_f = RTI[:, 8:24], RTI[:, 24:40], take(KT_), take(KT_)
            g = dve.add([slot_done], lambda e: e.tensor_scalar(g_i, slot_of[:, :], 7, None, ALU.logical_shift_right))
            r2 = dve.add([], lambda e: e.tensor_scalar(r_i, slot_of[:, :], P - 1, None, ALU.bitwise_and))
            g = dve.add([g], lambda e: e.tensor_copy(g_f, g_i))
            r2 = dve.add([r2], lambda e: e.tensor_copy(r_f, r_i))
            o1 = dve.add([g], lambda e: e.tensor_tensor(
                OHG[:, 0, :, :], bc(io_g, KT_), g_f.unsqueeze(2).to_broadcast([P, KT_, NT]), ALU.is_equal))
            o1b = act.add([o1], lambda e: e.activation(OHG[:, 1, :, :], OHG[:, 0, :, :], ACT.Copy, scale=pid))
            o2 = dve.add([o1], lambda e: e.tensor_tensor(
                OHG[:, 2, :, :], OHG[:, 0, :, :], tile_of.unsqueeze(2).to_broadcast([P, KT_, NT]), ALU.mult))
            o3 = dve.add([r2], lambda e: e.tensor_tensor(
                OHR[:, :, :], bc(io_r, KT_), r_f.unsqueeze(2).to_broadcast([P, KT_, P]), ALU.is_equal))
            tok_bank = 4
            for c in range(KT_):
                mm = pe.add([o1b, o2, o3, *free[tok_bank]], lambda e, c=c: e.matmul(
                    bank[tok_bank][:, 0:2 * NT].rearrange("p (a b) -> p a b", a=2), OHR[:, c, :], OHG[:, 1:3, c, :],
                    start=(c == 0), stop=(c == KT_ - 1)), mark=c == KT_ - 1)
            ge, ex_f = take(NT * NE).rearrange("p (a b) -> p a b", b=NE), take(NT)
            x = dve.add([a], lambda e: e.tensor_tensor(
                ge, io_g.unsqueeze(2).to_broadcast([P, NT, NE]), bc(last, NT), ALU.is_ge))
            x = dve.add([x], lambda e: e.tensor_reduce(ex_f, ge, AX, ALU.add))
            ex_done = dve.add([x, *rt_free["exp"]], lambda e: e.tensor_scalar(exp_of[:, :], ex_f, float(NE - 1), None, ALU.min))
            tk = take(2 * NT)
            y = dve.add([mm], lambda e: e.tensor_copy(tk, bank[tok_bank][:, 0:2 * NT]))
            free[tok_bank] = [y]
            tok_done = dve.add([y], lambda e: e.scalar_tensor_tensor(
                tok_of[:, :], tk[:, NT:2 * NT], float(P), tk[:, 0:NT], ALU.mult, ALU.add))
            s = dve.add([w], lambda e: e.tensor_reduce(ssum, ev, AX, ALU.add))
            s = dve.add([s], lambda e: e.reciprocal(srec, ssum))
            for k in range(TOPK):
                s1 = dve.add([s], lambda e, k=k: e.tensor_tensor(wts[:, k, :], ev[:, :, k], srec, ALU.mult))
            s = s1
            if layer == 1:
                ren, rec = take(8), take(8)
                s = dve.add([s], lambda e: e.tensor_tensor(ren, wts[:, 0, :], wts[:, 1, :], ALU.add))
                s = dve.add([s], lambda e: e.reciprocal(rec, ren))
                s = dve.add([s], lambda e: e.tensor_tensor(wts[:, :, :], wts[:, :, :], bc(rec, TOPK), ALU.mult))
                ps_, pk = sel.rearrange("p (a b) -> p a b", b=NE), slot_f
                s2 = dve.add([slot_done, ld_pes], lambda e: e.tensor_tensor(ps_, oh3, bc(pes[:, :], KT_), ALU.mult))
                s2 = dve.add([s2], lambda e: e.tensor_reduce(pk, ps_, AX, ALU.add))
                s = dve.add([s, s2], lambda e: e.tensor_tensor(
                    wts[:, :, :], wts[:, :, :], pk.rearrange("p (a b) -> p a b", a=TOPK), ALU.mult))
            return tok_done, ex_done, slot_done, s

        rt_free = {"exp": []}

        GX = [sb(f"GX{i}", [P, D]) for i in range(3)]
        gx_sem = [[counter(f"gx{l}_{i}") for i in range(3)] for l in range(2)]
        z_sem = [[counter(f"z{l}_{i}") for i in range(2)] for l in range(2)]

        def experts(layer, W1, W2, F, w1_ready, w2_ready, stored, tok_done, ex_done, r3_free, during=lambda: None):
            IC = F // P
            st = {}
            AH = 2 if layer else 1
            NH_ = AH + 1
            KB = F * 4 // 1024
            xsT = [view(R3, i, [DC, P]) for i in (0, 1, 12 if layer == 0 else 9)]
            H = [view(R3, 2 + KB * i, [F]) for i in range(NH_)]
            HT = [view(R3, 6 + KB * i, [IC, P]) for i in range(2)]
            Z = [view(R3, 10 + i, [D]) for i in range(2)]
            G2 = [view(R3, a_, [D]) for a_ in (12, 13, 5)][0:NH_]
            gx_free, xs_free, ht_free, h_free = ([list(r3_free) for _ in range(3)] for _ in range(4))
            z_free = [list(r3_free) for _ in range(2)]
            st["gathered"] = 0

            def gather_to(n):
                while st["gathered"] < min(n, NT):
                    gather(st["gathered"])
                    st["gathered"] += 1

            def gather(g):
                j = g % 3
                st["gx", g] = pool.dma([*stored, tok_done, *gx_free[j]], lambda e: e.indirect_dma_start(
                    GX[j][:, :], None, xn_dram[layer], bass.IndirectOffsetOnAxis(tok_of[:, g:g + 1], 0)),
                    gx_sem[layer][j])

            expert = {}

            def load_expert(g):
                def fn(e):
                    expert[g] = e.value_load(exp_of[0:1, g:g + 1], min_val=0, max_val=NE - 1)
                pe.add([ex_done], fn, mark=False)

            def turn_x(g):
                j, bk = g % 3, 4
                for dc in range(DC):
                    tr = pe.add([st["gx", g], *free[bk]], lambda e, dc=dc: e.transpose(
                        bank[bk][:, dc * P:(dc + 1) * P], GX[g % 3][:, dc * P:(dc + 1) * P], ident), mark=dc == DC - 1)
                gx_free[g % 3] = [tr]
                st["xs", g] = copy_on(act, [tr, *xs_free[j]], xsT[j],
                                      bank[bk][:, 0:D].rearrange("p (a b) -> p a b", a=DC))
                free[bk] = [st["xs", g]]
                gather_to(g + 4)

            def up_banks(g):
                if layer == 0:
                    k = 2 * (g % 2)
                    return [k, k + 1], bank[k], bank[k + 1]
                return [g % 4], bank[g % 4][:, 0:F], bank[g % 4][:, F:2 * F]

            def up(g):
                j, (bks, gate, _) = g % 3, up_banks(g)

                def one(e, n, dc):
                    return e.matmul(bank[bks[n]], xsT[j][:, dc, :],
                                    W1[:, dc, bass.ds(expert[g] * (2 * F) + n * 512, 512)],
                                    start=(dc == 0), stop=(dc == DC - 1))

                ms = []
                for n in range(len(bks)):
                    for dc in range(DC):
                        mm = pe.add([st["xs", g], ex_done, *w1_ready, *free[bks[n]]],
                                    lambda e, n=n, dc=dc: one(e, n, dc), mark=dc == DC - 1)
                    ms.append(mm)
                xs_free[j] = [mm]
                st["up", g] = ms
                if layer == 1:
                    u = G2[g % NH_]
                    a = act.add([ms[0], *h_free[g % NH_]], lambda e: e.activation(u, gate, ACT.Square))
                    a = dve.add([a], lambda e: e.tensor_scalar(
                        u, u, GELU_C * 0.044715, GELU_C, ALU.mult, ALU.add))
                    st["inner", g] = dve.add([a], lambda e: e.tensor_tensor(u, gate, u, ALU.mult))

            def activate(g):
                bks, gate, upv = up_banks(g)
                ms, h = st["up", g], H[g % NH_]
                if layer == 0:
                    a = act.add([ms[0], *h_free[g % NH_]], lambda e: e.activation(h, gate, ACT.Tanh, scale=0.5))
                else:
                    u = G2[g % NH_]
                    a = act.add([st["inner", g], *h_free[g % NH_]], lambda e: e.activation(h, u, ACT.Tanh))
                a = dve.add([a], lambda e: e.scalar_tensor_tensor(h, h, 1.0, gate, ALU.add, ALU.mult))
                a = dve.add([a, ms[-1]], lambda e: e.scalar_tensor_tensor(h, h, 0.5, upv, ALU.mult, ALU.mult))
                st["h", g] = a
                for b in bks:
                    free[b] = [a]

            def turn_h(g):
                j, bk, h = g % 2, 5 + g % 2, H[g % NH_]
                for ic in range(IC):
                    tr = pe.add([st["h", g], *free[bk]], lambda e, ic=ic: e.transpose(
                        bank[bk][:, ic * P:(ic + 1) * P], h[:, ic * P:(ic + 1) * P], ident), mark=ic == IC - 1)
                h_free[g % NH_] = [tr]
                st["ht", g] = copy_on(act, [tr, *ht_free[j]], HT[j],
                                      bank[bk][:, 0:F].rearrange("p (a b) -> p a b", a=IC))
                free[bk] = [st["ht", g]]

            def down(g):
                j, bk = g % 2, 7

                def one(e, ic):
                    return e.matmul(bank[bk][:, 0:D], HT[j][:, ic, :], W2[:, ic, bass.ds(expert[g] * D, D)],
                                    start=(ic == 0), stop=(ic == IC - 1))

                for ic in range(IC):
                    mm = pe.add([st["ht", g], *w2_ready, *free[bk]], lambda e, ic=ic: one(e, ic), mark=ic == IC - 1)
                ht_free[j] = [mm]
                zc = copy_on(dve, [mm, *z_free[j]], Z[j], bank[bk][:, 0:D])
                free[bk] = [zc]
                z_free[j] = [sp.dma([zc], lambda e: e.dma_start(ys_dram[layer][g * P:(g + 1) * P, :], Z[j]),
                                    z_sem[layer][j])]
                st["down"] = mm

            gather_to(3)
            load_expert(0)
            turn_x(0)
            for g in range(AH):
                load_expert(g + 1)
                turn_x(g + 1)
                up(g)
                if layer == 0 or g:
                    activate(g if layer == 0 else g - 1)
            load_expert(AH + 1)
            turn_x(AH + 1)
            for g in range(NT):
                if g + AH < NT:
                    up(g + AH)
                if g + 1 < NT:
                    activate(g + 1)
                if g + AH + 2 < NT:
                    load_expert(g + AH + 2)
                turn_h(g)
                if g + AH + 2 < NT:
                    turn_x(g + AH + 2)
                if g >= 1:
                    down(g - 1)
                if g == 4:
                    during()
            down(NT - 1)
            return xs_free[(NT - 1) % 3][0], st["down"], [z_sem[layer][i].token() for i in range(2)]

        YG = view(R2, 0, [TOPK * TT, D])
        yg_sem = [[counter(f"yg{l}_{c}") for c in range(TOPK * TT)] for l in range(2)]

        def combine(layer, z_tokens, slot_done, w_done, r2_free, finish, apply=lambda i: None):
            toks = {}

            def gather(i):
                for k in range(TOPK):
                    c = k * TT + i
                    toks[i, k] = pool.dma([*z_tokens, slot_done, *r2_free], lambda e, c=c: e.indirect_dma_start(
                        YG[:, c, :], None, ys_dram[layer], bass.IndirectOffsetOnAxis(slot_of[:, c:c + 1], 0)),
                        yg_sem[layer][c])

            def tile(i):
                tk = w_done
                for k in range(TOPK):
                    c = k * TT + i
                    tk = dve.add([toks[i, k], tk], lambda e, c=c, k=k: e.scalar_tensor_tensor(
                        X[:, i, :], YG[:, c, :], wts[:, k, i:i + 1], X[:, i, :], ALU.mult, ALU.add))
                finish(i, tk)
                if layer == 1 and i + 4 < TT:
                    gather(i + 4)
                if i % 4:
                    apply(i - 1)
                if i % 4 == 3:
                    apply(i)

            for i in range(4):
                gather(i)
            tile.gather = gather
            return tile

        store_sem = [[counter(f"store{l}_{i}") for i in range(TT)] for l in range(2)]

        def tile_steps(layer, rt, xn_free, xnT_free):
            stored, stats, normed, turned, factor = [], {}, {}, {}, {}

            def finish(i, x_ready):
                stats[i] = norm_stats(i, [x_ready])

            def apply(i):
                normed[i] = norm_apply(i, stats[i], xn_free)
                stored.append(sp.dma([normed[i]], lambda e: e.dma_start(
                    xn_dram[layer][i * P:(i + 1) * P, :], XN[:, i, :]), store_sem[layer][i]))

            def turn(i):
                tr, src = transpose_xn(i, 1, normed[i])
                turned[i] = copy_on(act, [tr, *xnT_free], xnT[:, :, i * P:(i + 1) * P], src)
                free[1] = [turned[i]]
                if layer == 1:
                    factor[i] = router_factor(i, normed[i], rt)

            def route(i):
                route_tile(layer, i, turned[i], factor.get(i), rt)

            return stored, finish, apply, turn, route

        rt0 = {"lg_free": [], "junk_free": []}
        w2 = view(R2, 0, [F0 // P, NE, D])
        ld_w2 = []

        def load_w2(i):
            if i in (3, 7):
                n = i // 4
                ld_w2.append(load(f"ld_w2_{n}", w2[:, 2 * n:2 * n + 2, :, :], t["w2"][:, 2 * n:2 * n + 2, :, :],
                                  [at0.q_done[i]]))

        stored0, *steps0 = tile_steps(0, rt0, [], [q0_last_mm])
        ckv1, wo1 = view(R4, 8, [NH, C]), view(R4, 12, [NH, D])
        ld_ckv1 = load("ld_ckv1", ckv1, t["ckv1"], [q0_last_mm])
        ld_wo1 = load("ld_wo1", wo1, t["wo1"], [q0_last_mm])
        at0.run(b_ready, *steps0, each=load_w2)
        tok_done, ex_done, slot_done, w_done = route(
            0, rt0["sorted"], lambda: output_matrices(ckv1, wo1, [ld_ckv1, ld_wo1], [at0.b_done], (act, act)))
        b1_ready, raw1_done = rt_extra[-1]
        w1f = view(R1, 0, [DC, NE * 2 * F0])
        w2f = view(R2, 0, [F0 // P, NE * D])

        r4_free = [rt0["sorted"], q0_last_mm, raw1_done]
        wq1, kcq1 = view(R4, 0, [NH, D]), view(R4, 16, [NH, QW])
        ld_raw1 = []

        def load_raw1():
            ld_raw1.append(load("ld_wq1", wq1, t["wq1"], r4_free))
            ld_raw1.append(load("ld_kcq1", kcq1, t["kcq1"], r4_free))

        up_done, down_done, z_tok = experts(0, w1f, w2f, F0, ld_w1, ld_w2, stored0, tok_done, ex_done,
                                            [at0.b_done, rt0["sorted"]], load_raw1)
        rt_free["exp"] = [down_done]

        NBK = 3
        CMH, CML = (v_[:, :].rearrange("p (a b c) -> p a b c", a=DC, b=NP) for v_ in (CMH_, CML_))
        TTm = view(R1, 48, [NP, NBK, P])
        qr1, kr1 = view(R2, 16, [NP, NBK * P]), view(R2, 28, [NP, P])
        ld_qr1 = load("ld_qr1", qr1, t["qr1"], [down_done])
        ld_kr1 = load("ld_kr1", kr1, t["kr1"], [down_done])

        def expand_matrices():
            toks = []
            for hp in range(NP):
                for dc in range(DC):
                    bk = (2 * hp + dc) % 4
                    wq_ = [wq1[:, 2 * hp + h2, dc * P:(dc + 1) * P] for h2 in range(2)]
                    k0, k1 = kcq1[:, 2 * hp, :], kcq1[:, 2 * hp + 1, :]
                    for out_, w_, x_ in (
                            (bank[bk].rearrange("p (a b) -> p a b", a=2)[:, :, 0:HQ], wq_[0],
                             k0.rearrange("p (a b) -> p a b", a=2)),
                            (bank[bk][:, HQ:2 * P], wq_[1], k1[:, 0:2 * P - HQ]),
                            (bank[bk][:, 2 * P + HQ:3 * P], wq_[1], k1[:, 2 * P - HQ:])):
                        mm = pe.add([*ld_raw1, *free[bk]], lambda e, out_=out_, w_=w_, x_=x_: e.matmul(
                            out_, w_, x_, start=True, stop=True))
                    toks.append(split(mm, CMH[:, dc, hp, :], CML[:, dc, hp, :], bank[bk][:, 0:3 * P], [bk], [up_done]))
            return toks

        def latent_matrices():
            toks = []
            for p in range(NP):
                bk = 4 + p % 4
                for j in range(NBK):
                    mm = pe.add([ld_qr1, ld_kr1, *free[bk]], lambda e, bk=bk, j=j, p=p: e.matmul(
                        bank[bk][:, j * P:(j + 1) * P], qr1[:, p, j * P:(j + 1) * P], kr1[:, p, :],
                        start=True, stop=True), mark=j == NBK - 1)
                tk = copy_on(act, [mm, up_done], TTm[:, p, :, :],
                             bank[bk][:, 0:NBK * P].rearrange("p (a b) -> p a b", a=NBK))
                free[bk] = [tk]
                toks.append(tk)
            return toks

        xnT1_ready, stats1, normed1 = {}, {}, {}

        def norm1_finish(i, x_ready):
            stats1[i] = norm_stats(i, [x_ready])

        def norm1_apply(i):
            normed1[i] = norm_apply(i, stats1[i], stored0)

        def turn_norm1(i):
            xnT1_ready[i] = split_xn(i, 6 + i % 2, normed1[i], [cm_ready[-1]])

        cm_ready = expand_matrices()
        combine_tile = combine(0, z_tok, slot_done, w_done, [down_done], norm1_finish, norm1_apply)
        for i in range(4):
            combine_tile(i)
        tt_ready = latent_matrices()
        for i in range(4):
            turn_norm1(i)

        RO = [view(R4, 16 + 6 * i, [NBK, 512]) for i in range(2)]
        PR = [view(R3, 8 + 6 * i, [NBK, 512]) for i in range(2)]
        pr_free = [list(b1_ready) + z_tok for _ in range(2)]
        ro_free = [[cm_ready[-1]] for _ in range(2)]
        q1_ready = {}
        LO, HI = slice(0, 64), slice(64, 128)

        def v3(ap):
            return ap.rearrange("p (a b) -> p a b", b=S)

        def tab(v, rows=slice(0, P)):
            return bc(ropeq[rows, v, :], 8)

        def roped_pair(n, hf, p):
            bks, ro, pr = [3 * (n % 2) + j for j in range(NBK)], RO[n % 2], PR[n % 2]
            mms = {}
            for j in (0, 2, 1):
                rows, cols = slice(j * P, (j + 1) * P), slice(hf * 512, (hf + 1) * 512)
                for dc in range(DC):
                    mm = product(bank[bks[j]], CMH[:, dc, p, rows], CML[:, dc, p, rows],
                                 XH[:, dc, cols], XL[:, dc, cols],
                                 [*cm_ready, *[xnT1_ready[i] for i in range(4 * hf, 4 * hf + 4)], *free[bks[j]]],
                                 dc == 0, dc == DC - 1)
                mms[j] = mm
            ALL = slice(0, P)
            for src, rs_, v, dst, rd in ((0, ALL, 0, ro[:, 0, :], ALL), (0, ALL, 3, pr[:, 2, :], ALL),
                                         (2, ALL, 1, pr[:, 0, :], ALL), (2, ALL, 2, ro[:, 2, :], ALL),
                                         (1, ALL, 4, ro[:, 1, :], ALL), (1, HI, 5, pr[:, 1, :], LO),
                                         (1, LO, 5, pr[:, 1, :], HI)):
                tk = dve.add([mms[src], ld_ropeq, *pr_free[n % 2], *ro_free[n % 2]],
                             lambda e, src=src, rs_=rs_, v=v, dst=dst, rd=rd: e.tensor_tensor(
                                 v3(dst[rd]), v3(bank[bks[src]][rs_]), tab(v, rs_), ALU.mult))
                free[bks[src]] = [tk]
            for j in (0, 2, 1):
                r = pool.add([tk], lambda e, j=j: e.tensor_tensor(ro[:, j, :], ro[:, j, :], pr[:, j, :], ALU.add))
            pr_free[n % 2] = [r]
            return r

        def latent_query(n, hf, p, roped):
            bk = 6 + n % 2
            for m, j in enumerate((0, 2, 1)):
                mm = pe.add([roped, *tt_ready, *free[bk]], lambda e, j=j, m=m: e.matmul(
                    bank[bk], TTm[:, p, j, :], RO[n % 2][:, j, :], start=(m == 0), stop=(m == 2)), mark=m == 2)
            q1_ready[p, hf] = copy_on(act, [mm, q_free], Q[:, hf, p, :], bank[bk])
            free[bk] = [q1_ready[p, hf]]
            ro_free[n % 2] = [mm]

        at1 = Attention(lambda i: [q1_ready[p, i // 4] for p in range(NP)], [b1_ready[-1], z_tok[0], z_tok[1]])
        n, todo = 0, []
        for hf in range(2):
            for p in range(NP):
                if hf == 0 and p < 4:
                    combine_tile.gather(4 + p)
                todo.append((n, hf, p, roped_pair(n, hf, p)))
                if hf == 0 and 1 <= p < 5:
                    combine_tile(3 + p)
                    q_free = (dve.sem, dve.count)
                if hf == 0 and p == 6:
                    for i in range(4, TT):
                        turn_norm1(i)
                if len(todo) == 2:
                    latent_query(*todo.pop(0))
                n += 1
                if (hf, p) == (1, 1):
                    at1.scores(0)
                    at1.exponential(0)
                if (hf, p) == (1, 2):
                    at1.normalise(0)
                if (hf, p) == (1, 4):
                    at1.scores(1)
                    at1.exponential(1)
                if (hf, p) == (1, 5):
                    at1.normalise(1)
        latent_query(*todo.pop(0))

        rope_done = (pe.sem, pe.count)
        g1 = view(R1, 0, [DC, NE * 2 * F1])
        l1 = view(R1, 32, [F1 // P, NE * D])
        ld_g1 = [load("ld_g1", g1, t["g1"], [rope_done])]
        ld_l1 = [load("ld_l1", l1, t["l1"], [rope_done])]

        rt1 = {"lg_free": [ex_done], "junk_free": []}
        for k in range(2):
            at1.et_free[k] = at1.ct_free[k] = [(pool.sem, pool.count), (dve.sem, dve.count)]
        stored1, *steps1 = tile_steps(1, rt1, [], [rope_done])
        at1.run(b1_ready, *steps1)
        tok1, ex1, slot1, w1_ = route(1, rt1["sorted"])
        up1, down1, z1 = experts(1, g1, l1, F1, ld_g1, ld_l1, stored1, tok1, ex1,
                                 [at1.b_done, rt1["sorted"], (act.sem, act.count)])
        out_sem = counter("out")

        def write_out(i, x_ready):
            sp.dma([x_ready], lambda e: e.dma_start(out[i * P:(i + 1) * P, :], X[:, i, :]), out_sem)

        combine_tile = combine(1, z1, slot1, w1_, [at1.q_done[TT - 1]], write_out)
        for i in range(TT):
            combine_tile(i)

        block = ctx.enter_context(nc.Block())

        @block.sync
        def _(e):
            sp.play(e)
            e.wait_ge(out_sem.sem, out_sem.count)

        @block.scalar
        def _(e):
            act.play(e)

        @block.vector
        def _(e):
            dve.play(e)

        @block.gpsimd
        def _(e):
            pool.play(e)

        @block.tensor
        def _(e):
            pe.play(e)


def tables():
    f = np.float32
    k, m = np.arange(P)[:, None], np.arange(P)[None, :]
    consts = np.stack([(k == m), (k < m), np.ones((P, P))], 1).astype(f)

    def rope(n, dim):
        inv = f(1.0) / np.power(f(10000.0), np.arange(0, dim, 2, dtype=f) / f(dim)).astype(f)
        fr = np.arange(n, dtype=f)[:, None] * inv[None, :]
        return np.repeat(np.sin(fr), 2, -1).astype(f), np.repeat(np.cos(fr), 2, -1).astype(f)

    sin, cos = rope(S, C)
    sign = np.where(np.arange(C) < C // 2, f(-1), f(1))
    ropek = np.concatenate([np.stack([cos, sin * sign], 1)] * 2, 0)
    sin, cos = rope(S, QW)
    q = np.arange(P) % HQ
    q1 = HQ - 64 + np.arange(64)
    ropeq = np.stack([cos[:, q].T, -sin[:, q].T, cos[:, q + HQ].T, sin[:, q + HQ].T,
                      np.concatenate([cos[:, q1].T, cos[:, q1 + HQ].T]),
                      np.concatenate([sin[:, q1 + HQ].T, -sin[:, q1].T])], 1)
    small = np.zeros((P, 512), f)
    small[:, 0:8] = np.arange(8)
    small[:, 8:136] = np.arange(P)
    small[:, 136:152] = np.tile(np.arange(TT), TOPK)
    small[:, 152:216] = (np.arange(8)[None, :] < np.arange(8)[:, None]).reshape(-1)
    small[:, 216:216 + NT] = np.arange(NT)
    small[:, 248] = np.arange(P)
    return {"consts": consts, "ropek": ropek, "ropeq": ropeq, "small": small}


def lay_out(i):
    a = {"x": i["x"].reshape(TT, P, D).transpose(1, 0, 2), "ctx": i["ctx_512"].transpose(1, 0, 2)}
    for l in range(2):
        def w(n):
            return i[f"L{l}_xattn_{n}"]
        kr = w("W_kr").reshape(NP, 2, C, 64).transpose(1, 3, 0, 2)
        a[f"kr{l}"] = np.zeros((P, NP, P), kr.dtype)
        for par in range(2):
            a[f"kr{l}"][64 * par:64 * par + 64, :, 64 * par:64 * par + 64] = kr[par]
        a[f"wq{l}"] = w("Wq").reshape(NH, HK, D).transpose(1, 0, 2)
        a[f"ckv{l}"] = w("w_kc_kv").transpose(1, 0, 2)
        a[f"wo{l}"] = w("Wo").reshape(D, NH, HK).transpose(2, 1, 0)
    a["kcq0"] = i["L0_xattn_w_kc_q"].reshape(NH, HK, 2, HQ).transpose(3, 2, 0, 1)
    qr0, qr1 = (i[f"L{l}_xattn_W_qr"].reshape(NP, 2, QW, 64).transpose(1, 3, 0, 2) for l in range(2))
    a["qr0"] = qr0.reshape(P, NP, QW)
    cut = P - HQ
    a["qr1"] = np.zeros((P, NP, 3 * P), qr1.dtype)
    a["qr1"][0:64, :, 0:HQ], a["qr1"][0:64, :, 2 * P:2 * P + HQ] = qr1[0][..., 0:HQ], qr1[0][..., HQ:QW]
    a["qr1"][64:, :, HQ:P], a["qr1"][64:, :, 2 * P + HQ:] = qr1[1][..., 0:cut], qr1[1][..., HQ:HQ + cut]
    a["qr1"][64:, :, P:P + 64], a["qr1"][64:, :, P + 64:2 * P] = qr1[1][..., cut:HQ], qr1[1][..., HQ + cut:]
    kcq1 = i["L1_xattn_w_kc_q"].transpose(1, 0, 2)
    a["kcq1"] = kcq1.copy()
    odd = kcq1[:, 1::2]
    a["kcq1"][:, 1::2] = np.concatenate(
        [odd[..., 0:cut], odd[..., cut:HQ], odd[..., HQ + cut:], odd[..., HQ:HQ + cut]], -1)
    a["w1"] = i["L0_ffn_w1"].reshape(NE, 2 * F0, DC, P).transpose(3, 2, 0, 1)
    a["w2"] = i["L0_ffn_w2"].reshape(NE, D, F0 // P, P).transpose(3, 2, 0, 1)
    a["g1"] = i["L1_ffn_gating_einsum"].reshape(NE, 2 * F1, DC, P).transpose(3, 2, 0, 1).reshape(P, DC, NE * 2 * F1)
    a["l1"] = i["L1_ffn_linear"].reshape(NE, F1 // P, P, D).transpose(2, 1, 0, 3).reshape(P, F1 // P, NE * D)
    a["rout"] = np.stack([i["L0_ffn_router_w"].reshape(NE, DC, P).transpose(2, 1, 0),
                          i["L1_ffn_router_logits"].reshape(DC, P, NE).transpose(1, 0, 2)], 1)
    a["rscale"] = i["L1_ffn_router_scale"].reshape(DC, P).T
    a["pes"] = np.broadcast_to(i["L1_ffn_per_expert_scale"], (P, NE))
    return a


def kernel(**inputs):
    import concourse.bacc as _bacc
    from concourse.bass_utils import run_bass_kernel_spmd as _run

    nc = _bacc.Bacc("TRN2", target_bir_lowering=False, num_devices=1)
    arrays, aps = {}, {}
    for name, a in {**lay_out({k: np.asarray(v) for k, v in inputs.items()}), **tables()}.items():
        arrays[f"in_{name}"] = np.ascontiguousarray(a)
        aps[name] = nc.dram_tensor(f"in_{name}", a.shape, mybir.dt.from_np(a.dtype), kind="ExternalInput").ap()
    out = nc.dram_tensor("out", [TOK, D], F32, kind="ExternalOutput").ap()
    build(nc, aps, out)
    r = _run(nc, [arrays], core_ids=[0])
    return r.results[0]["out"].reshape(NB, S, D)
```

```python
from contextlib import ExitStack

import numpy as np

import concourse.bass as bass
from concourse import mybir
from concourse.alu_op_type import AluOpType as ALU

F32 = mybir.dt.float32
F32R = mybir.dt.float32r
BF16 = mybir.dt.bfloat16
I32 = mybir.dt.int32
U32 = mybir.dt.uint32
ACT = mybir.ActivationFunctionType
AX = mybir.AxisListType.X

P = 128
NB, S = 16, 64
TOK = NB * S
TT = TOK // P
D = 256
DC = D // P
NH, HK = 16, 128
NP = NH // 2
C = 64
QW, HQ = 192, 96
NBLK = NH * HQ // P
NE, TOPK = 8, 2
NT = TOK * TOPK // P + NE - 1
NM = TOK * TOPK // P + NE // 2
F0, F1 = 512, 256
EPS = 1e-5
GELU_C = float(np.sqrt(2.0 / np.pi))


class Queue:

    def __init__(self, sem):
        self.sem, self.count, self.items = sem, 0, []

    def begin_if_more(self, waits, value, limit):
        self.outer, self.items = self.items, []
        self.condition = (waits, value, limit)
        self.before = self.count

    def end_if(self):
        body, self.items = self.items, self.outer
        self.items.append((self.condition, body, (self.before, self.count)))

    def add(self, waits, fn, mark=True):
        self.count += mark
        self.items.append((waits, fn, self.sem if mark else None, 1))
        return (self.sem, self.count)

    def dma(self, waits, fn, sem):
        sem.count += 16
        self.items.append((waits, fn, sem.sem, 16))
        return (sem.sem, sem.count)

    def play(self, eng, items=None, reached=()):
        reached = dict(reached)

        def wait(waits):
            for s, v in waits:
                if reached.get(id(s), 0) < v:
                    eng.wait_ge(s, v)
                    reached[id(s)] = v

        for item in self.items if items is None else items:
            if len(item) == 3:
                (waits, value, limit), body, (before, after) = item
                wait(waits)
                n = eng.value_load(value, min_val=0, max_val=NT)
                with eng.If(n > limit):
                    self.play(eng, body, reached)
                if after > before:
                    with eng.Else():
                        eng.wait_ge(self.sem, before)
                        eng.sem_inc(self.sem, after - before)
                continue
            waits, fn, sem, by = item
            wait(waits)
            ins = fn(eng)
            if sem is not None:
                ins.then_inc(sem, by)


class Counter:
    def __init__(self, sem):
        self.sem, self.count = sem, 0

    def token(self):
        return (self.sem, self.count)


def copy_on(queue, waits, out, in_):
    return queue.add(waits, lambda e: (e.copy if hasattr(e, "copy") else e.tensor_copy)(out, in_))


def build(nc, t, out):
    with ExitStack() as ctx:
        def sb(name, shape, dt=F32):
            return ctx.enter_context(nc.sbuf_tensor(name, shape, dt))

        def sem(name):
            return ctx.enter_context(nc.semaphore(name))

        def counter(name):
            return Counter(sem(name))

        sp, act, dve, pool, pe = (Queue(sem(n)) for n in ("s_sp", "s_act", "s_dve", "s_pool", "s_pe"))

        xn_dram = [nc.dram_tensor(f"xn_dram{i}", [TOK, D], F32).ap() for i in range(2)]
        ys_dram = [nc.dram_tensor(f"ys_dram{i}", [NT * P, D], F32).ap() for i in range(2)]

        X = sb("X", [P, TT, D])
        XN = sb("XN", [P, TT, D])
        VB = sb("VB", [P, NB, P])
        KT = sb("KT", [P, NB, P])
        B = sb("B", [P, NP, D])
        consts = sb("consts", [P, 3, P])
        ident, before, ones = (consts[:, i, :] for i in range(3))
        ropeq = sb("ropeq", [P, 6, S])
        small = sb("small", [P, 256])

        def under(*names_kb):
            with ExitStack() as now:
                return [now.enter_context(nc.sbuf_tensor(n, [P, kb * 256], F32R)) for n, kb in names_kb]

        AL_, = under(("A_lo", 8))
        CMH_, CML_ = under(("CM_hi", 24), ("CM_lo", 24))
        G1H_, G1L_ = under(("g1_hi", 32), ("g1_lo", 32))
        R1 = sb("R1", [P, 64 * 256])
        R2 = sb("R2", [P, 32 * 256])
        XSH_, XSL_ = under(("xs_hi", 3), ("xs_lo", 3))
        R3 = sb("R3", [P, 25 * 256])
        XTH_, XTL_, AH_ = under(("xnT_hi", 8), ("xnT_lo", 8), ("A_hi", 8))
        R4 = sb("R4", [P, 28 * 256])
        stat = sb("stat", [P, 64])
        before16, ones16 = sb("before16", [P, P], BF16), sb("ones16", [P, P], BF16)
        lnst = sb("lnst", [P, TT, 10])
        PSD = [ctx.enter_context(nc.psum_tensor(f"PSD{i}", [P, 2, 512], F32)) for i in range(4)]
        bank = [PSD[i // 2][:, i % 2, :] for i in range(8)]
        free = [[] for _ in range(8)]

        def view(region, at_kb, shape, parts=P, p0=0):
            n = int(np.prod(shape))
            v = region[p0:p0 + parts, at_kb * 256:at_kb * 256 + n]
            if len(shape) == 1:
                return v
            names = "abcd"[:len(shape)]
            return v.rearrange(f"p ({' '.join(names)}) -> p {' '.join(names)}",
                               **{k: s for k, s in zip(names[1:], shape[1:])})

        def load(name, dst, src, waits=()):
            return sp.dma(list(waits), lambda e: e.dma_start(dst, src), counter(name))

        qr0, kr0 = view(R4, 16, [NP, QW]), view(R4, 22, [NP, P])
        kcq0 = view(R1, 8, [2, NH, HK], parts=HQ)
        wq0, ckv0, wo0 = view(R1, 24, [NH, D]), view(R1, 40, [NH, C]), view(R1, 44, [NH, D])
        ctx_in = view(R3, 0, [NB, C])
        ctx_rope = view(R3, 4, [2, C])
        ctx_cos = view(R3, 5, [NB, C])
        ctx_sin = view(R3, 9, [NB, C])
        rout = sb("rout", [P, 2, DC, NE])
        rscale = sb("rscale", [P, DC])
        pes = sb("pes", [P, NE])
        ld_x, ld_kcq0, ld_wq0 = [], [], []
        ld_qr0 = load("ld_qr0", qr0, t["qr0"])
        ld_kr0 = load("ld_kr0", kr0, t["kr0"])
        for i in range(2):
            hs = slice(8 * i, 8 * i + 8)
            ld_x.append(load(f"ld_x{i}", X[:, 4 * i:4 * i + 4, :], t["x"][:, 4 * i:4 * i + 4, :]))
            if i == 0:
                ld_c = load("ld_consts", consts[:, :, :], t["consts"])
            ld_kcq0.append(load(f"ld_kcq0_{i}", kcq0[:, :, hs, :], t["kcq0"][:, :, hs, :]))
            ld_wq0.append(load(f"ld_wq0_{i}", wq0[:, hs, :], t["wq0"][:, hs, :]))
        ld_ctx = sp.dma([], lambda e: e.dma_start(ctx_in[0:64], t["ctx"]), counter("ld_ctx0"))
        ld_ctx2 = sp.dma([], lambda e: e.dma_start(ctx_in[64:128], t["ctx"]), counter("ld_ctx1"))
        ld_rk = load("ld_ropek", ctx_rope, t["ropek"])
        ld_ckv0 = load("ld_ckv0", ckv0, t["ckv0"])
        ld_wo0 = load("ld_wo0", wo0, t["wo0"])
        ld_small = load("ld_small", small[:, :], t["small"])
        ld_rout = load("ld_rout", rout[:, :, :, :], t["rout"])
        ld_rs = load("ld_rscale", rscale[:, :], t["rscale"])
        ld_pes = load("ld_pes", pes[:, :], t["pes"])
        ld_ropeq = load("ld_ropeq", ropeq[:, :, :], t["ropeq"])

        half_neg = stat[:, 0:1]
        z_half = pool.add([], lambda e: e.memset(half_neg, -0.5))

        def norm_stats(tile, waits):
            bn, mv, ve = lnst[:, tile, 0:6], lnst[:, tile, 6:8], lnst[:, tile, 8:9]
            a = dve.add(list(waits), lambda e: e.bn_stats(bn, X[:, tile, :]))
            a = dve.add([a], lambda e: e.bn_aggr(mv, bn))
            a = dve.add([a], lambda e: e.tensor_scalar(ve, mv[:, 1:2], EPS, None, ALU.add))
            return pool.add([a, z_half], lambda e: e.tensor_tensor(lnst[:, tile, 9:10], ve, half_neg, ALU.pow))

        def norm_apply(tile, stats, waits=()):
            return dve.add([stats, *waits], lambda e: e.tensor_scalar(
                XN[:, tile, :], X[:, tile, :], lnst[:, tile, 6:7], lnst[:, tile, 9:10], ALU.subtract, ALU.mult))

        def transpose_xn(tile, b, xn_ready):
            for dc in range(DC):
                tr = pe.add([xn_ready, ld_c, *free[b]], lambda e, dc=dc: e.transpose(
                    bank[b][:, dc * P:(dc + 1) * P], XN[:, tile, dc * P:(dc + 1) * P], ident), mark=dc == DC - 1)
            return tr, bank[b][:, 0:DC * P].rearrange("p (a b) -> p a b", a=DC)

        def split(ready, hi, lo, src, banks, waits=()):
            a = act.add([ready, *waits], lambda e: e.copy(hi, src))
            a = dve.add([a], lambda e: e.tensor_tensor(lo, src, hi.bitcast(F32), ALU.subtract))
            for b in banks:
                free[b] = [a]
            return a

        def product(out, wh, wl, xh, xl, waits, first, last):
            for i, (w_, x_) in enumerate(((wh, xh), (wh, xl), (wl, xh))):
                mm = pe.add(waits, lambda e, i=i, w_=w_, x_=x_: e.matmul(
                    out, w_, x_, start=first and i == 0, stop=last and i == 2), mark=last and i == 2)
            return mm

        def split_xn(tile, b, xn_ready, waits=()):
            tr, src = transpose_xn(tile, b, xn_ready)
            cols = slice(tile * P, (tile + 1) * P)
            return split(tr, XH[:, :, cols], XL[:, :, cols], src, [b], waits)

        H2 = C // 2

        def bc(ap, n):
            return ap.unsqueeze(1).to_broadcast([ap.shape[0], n, ap.shape[1]])

        zv = pool.add([], lambda e: e.memset(VB[:, :, :], 0.0))

        XH, XL = (v_[:, :].rearrange("p (a b) -> p a b", a=DC) for v_ in (XTH_, XTL_))
        xnT = view(R4, 0, [DC, TOK])
        T1 = view(R3, 13, [2, NH, C], parts=HQ)
        T2 = view(R3, 21, [NH, C])
        AH, AL = (v_[:, :].rearrange("p (a b) -> p a b", a=DC) for v_ in (AH_, AL_))
        t1_ready, t2_ready, a_ready, xnT_ready = {}, {}, {}, []

        def first_products(hh):
            for c in range(2):
                bk = 2 + 2 * hh + c
                for p4 in range(4):
                    p = 4 * hh + p4
                    mm = pe.add([ld_qr0, ld_kr0, *free[bk]], lambda e, bk=bk, c=c, p=p, p4=p4: e.matmul(
                        bank[bk][0:HQ, p4 * P:(p4 + 1) * P], qr0[:, p, c * HQ:(c + 1) * HQ], kr0[:, p, :],
                        start=True, stop=True), mark=p4 == 3)
                tk = copy_on(act, [mm], T1[:, c, 8 * hh:8 * hh + 8, :],
                             bank[bk][0:HQ, :].rearrange("p (a b) -> p a b", a=8))
                free[bk] = [tk]
                t1_ready[hh, c] = tk

        def second_products(hh):
            bk = hh
            for h8 in range(8):
                h = 8 * hh + h8
                for c in range(2):
                    mm = pe.add([ld_kcq0[hh], t1_ready[hh, 0], t1_ready[hh, 1], *free[bk]],
                                lambda e, bk=bk, h=h, h8=h8, c=c: e.matmul(
                                    bank[bk][:, h8 * C:(h8 + 1) * C], kcq0[:, c, h, :], T1[:, c, h, :],
                                    start=(c == 0), stop=(c == 1)), mark=(h8 == 7 and c == 1))
            tk = copy_on(act, [mm], T2[:, 8 * hh:8 * hh + 8, :], bank[bk].rearrange("p (a b) -> p a b", a=8))
            free[bk] = [tk]
            t2_ready[hh] = tk

        def third_products(hh):
            for dc in range(DC):
                bk = 2 + 2 * dc + hh
                for h8 in range(8):
                    h = 8 * hh + h8
                    mm = pe.add([ld_wq0[hh], t2_ready[hh], *free[bk]], lambda e, bk=bk, h=h, h8=h8, dc=dc: e.matmul(
                        bank[bk][:, h8 * C:(h8 + 1) * C], wq0[:, h, dc * P:(dc + 1) * P], T2[:, h, :],
                        start=True, stop=True), mark=h8 == 7)
                cols = slice(512 * hh, 512 * hh + 512)
                a_ready[hh, dc] = split(mm, AH[:, dc, cols], AL[:, dc, cols], bank[bk], [bk])

        def first_norm(tiles):
            stats = [norm_stats(i, [ld_x[i // 4]]) for i in tiles]
            normed = [norm_apply(i, s_) for i, s_ in zip(tiles, stats)]
            for i, xn in zip(tiles, normed):
                xnT_ready.append(split_xn(i, 6 + i % 2, xn))

        first_products(0)
        first_products(1)
        first_norm(range(4))
        second_products(0)
        first_norm(range(4, 8))
        third_products(0)
        second_products(1)

        a = dve.add([ld_ctx, ld_ctx2, ld_rk], lambda e: e.tensor_tensor(
            ctx_cos, ctx_in, bc(ctx_rope[:, 0, :], NB), ALU.mult))
        b_ = dve.add([], lambda e: e.tensor_tensor(ctx_sin[:, :, 0:H2], ctx_in[:, :, H2:C],
                                                   bc(ctx_rope[:, 1, 0:H2], NB), ALU.mult))
        b_ = dve.add([], lambda e: e.tensor_tensor(ctx_sin[:, :, H2:C], ctx_in[:, :, 0:H2],
                                                   bc(ctx_rope[:, 1, H2:C], NB), ALU.mult))
        for par in range(2):
            h = slice(64 * par, 64 * par + 64)
            vb_ready = dve.add([b_, zv], lambda e, h=h: e.tensor_tensor(
                VB[h, :, h], ctx_cos[h], ctx_sin[h], ALU.add))
        kt_ready = []

        def turn_context():
            for i in range(4):
                bk = 6 + i % 2
                for j in range(4):
                    tr = pe.add([vb_ready, *free[bk]], lambda e, bk=bk, i=i, j=j: e.transpose(
                        bank[bk][:, j * P:(j + 1) * P], VB[:, 4 * i + j, :], ident), mark=j == 3)
                tk = copy_on(act if i % 2 else dve, [tr], KT[:, 4 * i:4 * i + 4, :],
                             bank[bk].rearrange("p (a b) -> p a b", a=4))
                free[bk] = [tk]
                kt_ready.append(tk)

        def output_matrices(ckv, wo, waits, b_waits, engines):
            toks = []
            for i in range(4):
                bk = 2 + i
                for p2 in range(2):
                    for par in range(2):
                        h = 4 * i + 2 * p2 + par
                        mm = pe.add([*waits, *free[bk]], lambda e, bk=bk, h=h, p2=p2, par=par: e.matmul(
                            bank[bk][64 * par:64 * par + 64, p2 * D:(p2 + 1) * D], ckv[:, h, :], wo[:, h, :],
                            start=True, stop=True), mark=(p2 == 1 and par == 1))
                tk = copy_on(engines[i % 2], [mm, *b_waits], B[:, 2 * i:2 * i + 2, :],
                             bank[bk].rearrange("p (a b) -> p a b", a=2))
                free[bk] = [tk]
                toks.append(tk)
            return toks, mm

        Q = view(R2, 0, [2, NP, TOK // 2])
        q_ready = {}
        turn_q = [0]

        def latent_queries0(hf, hh):
            toks = []
            for p in range(4 * hh, 4 * hh + 4):
                bk = turn_q[0] % 4
                turn_q[0] += 1
                rows, cols = slice(p * P, (p + 1) * P), slice(hf * 512, (hf + 1) * 512)
                for dc in range(DC):
                    mm = product(bank[bk], AH[:, dc, rows], AL[:, dc, rows], XH[:, dc, cols], XL[:, dc, cols],
                                 [a_ready[hh, 0], a_ready[hh, 1], *xnT_ready[4 * hf:4 * hf + 4], *free[bk]],
                                 dc == 0, dc == DC - 1)
                toks.append(copy_on(act if p % 2 else dve, [mm], Q[:, hf, p, :], bank[bk]))
                free[bk] = [toks[-1]]
            q_ready[hf, hh] = toks

        latent_queries0(0, 0)
        third_products(1)
        turn_context()
        latent_queries0(0, 1)

        class Attention:

            def __init__(self, q_ready, r3_free):
                self.q_ready = q_ready
                self.E = [view(R3, 4 * i, [NH, S]) for i in range(2)]
                self.ET = [view(R3, 8 + 4 * i, [NP, P]) for i in range(2)]
                self.CT = [view(R3, 16 + 4 * i, [NP, P]) for i in range(2)]
                self.mx, self.sm, self.rs = ([sbm[:, 32 * k + 16 * i:32 * k + 16 * i + 16] for i in range(2)]
                                             for k in range(3))
                self.e_free = [list(r3_free), list(r3_free)]
                self.et_free = [list(r3_free), list(r3_free)]
                self.ct_free = [list(r3_free), list(r3_free)]
                self.e, self.sub, self.et, self.ct, self.q_done = {}, {}, {}, {}, {}

            def pair(self, k):
                return k, [*free[2 * k], *free[2 * k + 1]]

            def scores(self, i, k=2, pairs=range(NP)):
                for p in pairs:
                    for b2 in range(2):
                        b = 2 * i + b2
                        mm = pe.add([*self.q_ready(i), *kt_ready, *free[2 * k + p // 4]], lambda e, p=p, b=b, b2=b2: e.matmul(
                            bank[2 * k + p // 4][64 * b2:64 * b2 + 64, (p % 4) * P:(p % 4 + 1) * P],
                            Q[:, i // 4, p, (b % 8) * S:(b % 8 + 1) * S], KT[:, b, :], start=True, stop=True),
                            mark=(p == pairs[-1] and b2 == 1))
                self.q_done[i] = mm
                E, mx = self.E[i % 2], self.mx[i % 2]
                ps = PSD[k][:, :, :].rearrange("p a (h l) -> p (a h) l", l=S)
                m = dve.add([mm, *self.e_free[i % 2]], lambda e: e.tensor_reduce(mx, ps, AX, ALU.max))
                self.sub[i] = dve.add([m], lambda e: e.tensor_tensor(
                    E, ps, mx.unsqueeze(2).to_broadcast([P, NH, S]), ALU.subtract))
                free[2 * k] = free[2 * k + 1] = [self.sub[i]]

            def exponential(self, i):
                E = self.E[i % 2]
                self.e[i] = act.add([self.sub[i]], lambda e: e.activation(E, E, ACT.Exp))

            def normalise(self, i):
                E, sm, rs = self.E[i % 2], self.sm[i % 2], self.rs[i % 2]
                s = dve.add([self.e[i]], lambda e: e.tensor_reduce(sm, E, AX, ALU.add))
                s = dve.add([s], lambda e: e.reciprocal(rs, sm))
                self.e[i] = pool.add([s], lambda e: e.tensor_tensor(
                    E, E, rs.unsqueeze(2).to_broadcast([P, NH, S]), ALU.mult))

            def turn_weights(self, i):
                (k, k_free), j = self.pair(1), i % 2
                for p in range(NP):
                    tr = pe.add([self.e[i], *k_free], lambda e, p=p: e.transpose(
                        bank[2 * k + p // 4][:, (p % 4) * P:(p % 4 + 1) * P],
                        self.E[j][:, 2 * p:2 * p + 2, :].rearrange("p a b -> p (a b)"), ident), mark=p == NP - 1)
                self.e_free[j] = [tr]
                self.et[i] = copy_on(act, [tr, *self.et_free[j]], self.ET[j],
                                     PSD[k][:, :, :].rearrange("p a (h l) -> p (a h) l", l=P))
                free[2 * k] = free[2 * k + 1] = [self.et[i]]

            def weighted_context(self, i):
                (k, k_free), j = self.pair(3), i % 2
                self.ct[i] = []
                for b2 in range(2):
                    mm = pe.add([self.et[i], *k_free], lambda e, b2=b2: e.matmul(
                        bank[2 * k + b2], VB[:, 2 * i + b2, :], self.ET[j][:, :, b2 * S:(b2 + 1) * S],
                        start=True, stop=True))
                    tk = copy_on(act if b2 else dve, [mm, *self.ct_free[j]], self.CT[j][:, :, b2 * S:(b2 + 1) * S],
                                 bank[2 * k + b2].rearrange("p (a b) -> p a b", b=S))
                    free[2 * k + b2] = [tk]
                    self.ct[i].append(tk)
                self.et_free[j] = [mm]

            def project(self, i, b_ready, finish):
                k, j = 0, i % 2
                for p in range(NP):
                    mm = pe.add([*self.ct[i], *b_ready, *free[2 * k]], lambda e, p=p: e.matmul(
                        bank[2 * k][:, 0:D], self.CT[j][:, p, :], B[:, p, :], start=(p == 0), stop=(p == NP - 1)),
                        mark=p == NP - 1)
                self.ct_free[j] = [mm]
                self.b_done = mm
                tk = dve.add([mm], lambda e: e.tensor_tensor(X[:, i, :], bank[2 * k][:, 0:D], X[:, i, :], ALU.add))
                free[2 * k] = [tk]
                finish(i, tk)

            def run(self, b_ready, finish, apply, turn, route, each=lambda i: None):
                for i in range(TT + 3):
                    if i < TT:
                        self.turn_weights(i)
                    if i + 2 < TT:
                        self.scores(i + 2)
                        self.exponential(i + 2)
                    if 0 <= i - 2 < TT:
                        apply(i - 2)
                    if 0 <= i - 3 < TT:
                        turn(i - 3)
                    if i < TT:
                        self.weighted_context(i)
                    if i + 2 < TT:
                        self.normalise(i + 2)
                        each(i + 2)
                    if 0 <= i - 1 < TT:
                        self.project(i - 1, b_ready, finish)
                    if 0 <= i - 3 < TT:
                        route(i - 3)

        sbm = sb("sbm", [P, 96])

        at0 = Attention(lambda i: [*q_ready[i // 4, 0], *q_ready[i // 4, 1]],
                        [a_ready[1, 0], a_ready[1, 1], vb_ready])
        at0.scores(0, 2)
        at0.exponential(0)
        latent_queries0(1, 0)
        at0.normalise(0)
        latent_queries0(1, 1)
        q0_last_mm = (pe.sem, pe.count)
        at0.scores(1, 3)
        at0.exponential(1)
        b_ready, raw0_done = output_matrices(ckv0, wo0, [ld_ckv0, ld_wo0], [], (act, dve))
        at0.normalise(1)

        w1 = view(R1, 0, [DC, NE, 2 * F0])
        ld_w1 = [load(f"ld_w1_{i}", w1[:, i, :, :], t["w1"][:, i, :, :], [raw0_done]) for i in range(DC)]

        io_e, io_r = small[:, 0:8], small[:, 8:136]
        tile_of = small[:, 136:152]
        tri_e = small[:, 152:216].rearrange("p (a b) -> p a b", a=NE)
        io_g, pid = small[:, 216:216 + NT], small[:, 248:249]
        dve.add([ld_c], lambda e: e.tensor_copy(before16[:, :], before))
        bf16_ready = dve.add([], lambda e: e.tensor_copy(ones16[:, :], ones))
        rout1_ready = [dve.add([ld_rs, ld_rout], lambda e, dc=dc: e.tensor_scalar(
            rout[:, 1, dc, :], rout[:, 1, dc, :], rscale[:, dc:dc + 1], None, ALU.mult)) for dc in range(DC)]

        LG = sb("LG", [P, TT, NE])
        VAL = sb("VAL", [P, TT, 8])
        IDX = sb("IDX", [P, TT, 8], U32)
        RT = view(R3, 14, [1024])
        RTI = sb("RTI", [P, 96], I32)
        OHR = R3[:, 18 * 256:22 * 256].bitcast(BF16).rearrange("p (a b) -> p a b", b=P)
        OHG = R3[:, 22 * 256:22 * 256 + 3 * TOPK * TT * NT // 2].bitcast(BF16).rearrange(
            "p (v a b) -> p v a b", v=3, b=NT)
        tiles_of = sb("tiles_of", [P, 1], I32)
        tok_of = sb("tok_of", [P, NT], I32)
        slot_of = sb("slot_of", [P, TOPK * TT], I32)
        exp_of = sb("exp_of", [P, NT], I32)
        wts = sb("wts", [P, TOPK, TT])
        rms = sb("rms", [P, 3, TT])

        def router_factor(i, xn_ready, rt):
            ms, me, mr = (rms[:, n, i:i + 1] for n in range(3))
            junk = view(R3, 24, [D])
            a = act.add([xn_ready, *rt["junk_free"]], lambda e: e.activation(
                junk, XN[:, i, :], ACT.Square, accum_out=ms))
            rt["junk_free"] = [a]
            a = dve.add([a], lambda e: e.tensor_scalar(me, ms, 1.0 / D, 1e-6, ALU.mult, ALU.add))
            return pool.add([a], lambda e: e.tensor_tensor(mr, me, half_neg, ALU.pow))

        def route_tile(layer, i, xnT_done, factor, rt):
            bk = 6
            for dc in range(DC):
                mm = pe.add([xnT_done, ld_rout, *rout1_ready, *free[bk]], lambda e, dc=dc: e.matmul(
                    bank[bk][:, 0:NE], rt_xnT[:, dc, i * P:(i + 1) * P], rout[:, layer, dc, :],
                    start=(dc == 0), stop=(dc == DC - 1)), mark=dc == DC - 1)
            if layer == 0:
                lg = dve.add([mm, *rt["lg_free"]], lambda e: e.tensor_copy(LG[:, i, :], bank[bk][:, 0:NE]))
            else:
                lg = dve.add([factor, mm, *rt["lg_free"]], lambda e: e.tensor_scalar(
                    LG[:, i, :], bank[bk][:, 0:NE], rms[:, 2, i:i + 1], float(D) ** -0.5, ALU.mult, ALU.mult))
            free[bk] = [lg]
            v = dve.add([lg], lambda e: e.max(VAL[:, i, :], LG[:, i, :]))
            rt["sorted"] = dve.add([v], lambda e: e.max_index(IDX[:, i, :], VAL[:, i, :], LG[:, i, :]))

        rt_xnT = xnT

        rt_extra = []

        def route(layer, srt, meanwhile=lambda: None):
            n = [0]

            def take(k):
                v = RT[:, n[0]:n[0] + k]
                n[0] += k
                return v

            KT_ = TOPK * TT
            ev, ssum, srec = take(64).rearrange("p (a b) -> p a b", a=TT), take(8), take(8)
            w = dve.add([srt], lambda e: e.tensor_tensor(
                ev, VAL[:, :, :], VAL[:, :, 0:1].to_broadcast([P, TT, 8]), ALU.subtract))
            w = act.add([w], lambda e: e.activation(ev, ev, ACT.Exp))
            idf = take(KT_).rearrange("p (a b) -> p a b", a=TOPK)
            oh = take(KT_ * NE)
            oh3 = oh.rearrange("p (a b) -> p a b", b=NE)
            m = take(32).bitcast(BF16)
            for k in range(TOPK):
                a = dve.add([], lambda e, k=k: e.tensor_copy(idf[:, k, :], IDX[:, :, k]))
            a = dve.add([a, ld_small], lambda e: e.tensor_tensor(
                oh3, bc(io_e, KT_), idf.rearrange("p a b -> p (a b)").unsqueeze(2).to_broadcast([P, KT_, NE]),
                ALU.is_equal))
            a = dve.add([a], lambda e: e.tensor_tensor(m, oh[:, 0:64], oh[:, 64:128], ALU.add))
            rank_bank = 0
            pe.add([a, bf16_ready, *free[rank_bank]], lambda e: e.matmul(bank[rank_bank][:, 0:64], before16[:, :], m, start=True, stop=False,
                                                      skip_group_check=True), mark=False)
            for i in range(TT):
                mm = pe.add([], lambda e, i=i: e.matmul(
                    bank[rank_bank][:, 8 * (i + 1):8 * (TT + 1)].rearrange("p (a b) -> p a b", b=NE), ones16[:, :],
                    bc(m[:, 8 * i:8 * i + 8], TT - i), start=False, stop=(i == TT - 1),
                    skip_group_check=True), mark=i == TT - 1)
            rank = take(72)
            r = dve.add([mm], lambda e: e.tensor_copy(rank, bank[rank_bank][:, 0:72]))
            free[rank_bank] = [r]
            rt_extra.append(meanwhile())
            cnt_i, nt_f, prod = RTI[:, 0:8], take(8), take(64).rearrange("p (a b) -> p a b", a=NE)
            first, last, base = take(8), take(8), take(64).rearrange("p (a b) -> p a b", a=TT)
            a = dve.add([r], lambda e: e.tensor_scalar(cnt_i, rank[:, 64:72], float(P - 1), None, ALU.add))
            a = dve.add([a], lambda e: e.tensor_scalar(cnt_i, cnt_i, 7, None, ALU.logical_shift_right))
            a = dve.add([a], lambda e: e.tensor_copy(nt_f, cnt_i))
            a = dve.add([a], lambda e: e.tensor_tensor(prod, tri_e, bc(nt_f, NE), ALU.mult))
            a = dve.add([a], lambda e: e.tensor_reduce(first, prod, AX, ALU.add))
            a = dve.add([a], lambda e: e.tensor_tensor(last, first, nt_f, ALU.add))
            dve.add([a], lambda e: e.tensor_copy(tiles_of[:, :], last[:, NE - 1:NE]))
            a1 = dve.add([], lambda e: e.scalar_tensor_tensor(
                base, bc(first, TT), float(P), rank[:, 0:64].rearrange("p (a b) -> p a b", a=TT),
                ALU.mult, ALU.add))
            sel, slot_f = take(KT_ * NE), take(KT_)
            a1 = dve.add([a1], lambda e: e.tensor_tensor(
                sel.rearrange("p (k x) -> p k x", k=TOPK), oh.rearrange("p (k x) -> p k x", k=TOPK),
                bc(base.rearrange("p a b -> p (a b)"), TOPK), ALU.mult))
            a1 = dve.add([a1], lambda e: e.tensor_reduce(slot_f, sel.rearrange("p (a b) -> p a b", b=NE), AX, ALU.add))
            slot_done = dve.add([a1], lambda e: e.tensor_copy(slot_of[:, :], slot_f))
            g_i, r_i, g_f, r_f = RTI[:, 8:24], RTI[:, 24:40], take(KT_), take(KT_)
            g = dve.add([slot_done], lambda e: e.tensor_scalar(g_i, slot_of[:, :], 7, None, ALU.logical_shift_right))
            r2 = dve.add([], lambda e: e.tensor_scalar(r_i, slot_of[:, :], P - 1, None, ALU.bitwise_and))
            g = dve.add([g], lambda e: e.tensor_copy(g_f, g_i))
            r2 = dve.add([r2], lambda e: e.tensor_copy(r_f, r_i))
            o1 = dve.add([g], lambda e: e.tensor_tensor(
                OHG[:, 0, :, :], bc(io_g, KT_), g_f.unsqueeze(2).to_broadcast([P, KT_, NT]), ALU.is_equal))
            o1b = act.add([o1], lambda e: e.activation(OHG[:, 1, :, :], OHG[:, 0, :, :], ACT.Copy, scale=pid))
            o2 = dve.add([o1], lambda e: e.tensor_tensor(
                OHG[:, 2, :, :], OHG[:, 0, :, :], tile_of.unsqueeze(2).to_broadcast([P, KT_, NT]), ALU.mult))
            o3 = dve.add([r2], lambda e: e.tensor_tensor(
                OHR[:, :, :], bc(io_r, KT_), r_f.unsqueeze(2).to_broadcast([P, KT_, P]), ALU.is_equal))
            tok_bank = 4
            for c in range(KT_):
                mm = pe.add([o1b, o2, o3, *free[tok_bank]], lambda e, c=c: e.matmul(
                    bank[tok_bank][:, 0:2 * NT].rearrange("p (a b) -> p a b", a=2), OHR[:, c, :], OHG[:, 1:3, c, :],
                    start=(c == 0), stop=(c == KT_ - 1)), mark=c == KT_ - 1)
            ge, ex_f = take(NT * NE).rearrange("p (a b) -> p a b", b=NE), take(NT)
            x = dve.add([a], lambda e: e.tensor_tensor(
                ge, io_g.unsqueeze(2).to_broadcast([P, NT, NE]), bc(last, NT), ALU.is_ge))
            x = dve.add([x], lambda e: e.tensor_reduce(ex_f, ge, AX, ALU.add))
            ex_done = dve.add([x, *rt_free["exp"]], lambda e: e.tensor_scalar(exp_of[:, :], ex_f, float(NE - 1), None, ALU.min))
            tk = take(2 * NT)
            y = dve.add([mm], lambda e: e.tensor_copy(tk, bank[tok_bank][:, 0:2 * NT]))
            free[tok_bank] = [y]
            tok_done = dve.add([y], lambda e: e.scalar_tensor_tensor(
                tok_of[:, :], tk[:, NT:2 * NT], float(P), tk[:, 0:NT], ALU.mult, ALU.add))

            def weigh():
                s = dve.add([w], lambda e: e.tensor_reduce(ssum, ev, AX, ALU.add))
                s = dve.add([s], lambda e: e.reciprocal(srec, ssum))
                for k in range(TOPK):
                    s1 = dve.add([s], lambda e, k=k: e.tensor_tensor(wts[:, k, :], ev[:, :, k], srec, ALU.mult))
                s = s1
                if layer == 1:
                    ren, rec = take(8), take(8)
                    s = dve.add([s], lambda e: e.tensor_tensor(ren, wts[:, 0, :], wts[:, 1, :], ALU.add))
                    s = dve.add([s], lambda e: e.reciprocal(rec, ren))
                    s = dve.add([s], lambda e: e.tensor_tensor(wts[:, :, :], wts[:, :, :], bc(rec, TOPK), ALU.mult))
                    ps_, pk = sel.rearrange("p (a b) -> p a b", b=NE), slot_f
                    s2 = dve.add([slot_done, ld_pes], lambda e: e.tensor_tensor(ps_, oh3, bc(pes[:, :], KT_), ALU.mult))
                    s2 = dve.add([s2], lambda e: e.tensor_reduce(pk, ps_, AX, ALU.add))
                    s = dve.add([s, s2], lambda e: e.tensor_tensor(
                        wts[:, :, :], wts[:, :, :], pk.rearrange("p (a b) -> p a b", a=TOPK), ALU.mult))
                return s

            return tok_done, ex_done, slot_done, weigh

        rt_free = {"exp": []}

        GX = [sb(f"GX{i}", [P, D]) for i in range(3)]
        gx_sem = [[counter(f"gx{l}_{i}") for i in range(6)] for l in range(2)]
        z_sem = [[counter(f"z{l}_{i}") for i in range(4)] for l in range(2)]

        spare_rows = [sp.dma([vb_ready], lambda e, l=l: e.dma_start(
            ys_dram[l][NM * P:, :].rearrange("(a p) d -> p a d", p=P),
            VB[:, 0:DC * (NT - NM), :].rearrange("p (a b) c -> p a (b c)", b=DC)), counter(f"spare{l}")) for l in range(2)]

        def experts(layer, W1, W2, F, w1_ready, w2_ready, stored, tok_done, ex_done, r3_free, during):
            IC = F // P
            st = {}
            AH = 2 if layer else 1
            NH_ = AH + 1
            if layer == 0:
                xsT = [view(R3, i, [DC, P]) for i in (0, 1, 12)]
                h_at, ht_at, z_at, g2_at = (2, 4), (6, 8), (10, 11), ()
            else:
                xsT = [[v_[:, i * D:(i + 1) * D].rearrange("p (a b) -> p a b", a=DC) for v_ in (XSH_, XSL_)]
                       for i in range(3)]
                h_at, ht_at, z_at, g2_at = (6, 7, 8), (9, 10), (11, 12), (18, 19, 20)
            H = [view(R3, i, [F]) for i in h_at]
            HT = [view(R3, i, [IC, P]) for i in ht_at]
            Z = [view(R3, i, [D]) for i in z_at]
            G2 = [view(R3, i, [D]) for i in g2_at]
            gx_free, xs_free, ht_free, h_free = ([list(r3_free) for _ in range(3)] for _ in range(4))
            z_free = [list(r3_free) for _ in range(2)]
            st["gathered"] = 0

            def gather_to(n):
                while st["gathered"] < min(n, st["end"]):
                    gather(st["gathered"])
                    st["gathered"] += 1

            def gather(g):
                j = g % 3
                st["gx", g] = pool.dma([*stored, tok_done, *gx_free[j]], lambda e: e.indirect_dma_start(
                    GX[j][:, :], None, xn_dram[layer], bass.IndirectOffsetOnAxis(tok_of[:, g:g + 1], 0)),
                    gx_sem[layer][j + (3 if g >= NM else 0)])

            expert = {}

            def load_expert(g):
                def fn(e):
                    expert[g] = e.value_load(exp_of[0:1, g:g + 1], min_val=0, max_val=NE - 1)
                pe.add([ex_done], fn, mark=False)

            def turn_x(g):
                j, bk = g % 3, 4
                for dc in range(DC):
                    tr = pe.add([st["gx", g], *free[bk]], lambda e, dc=dc: e.transpose(
                        bank[bk][:, dc * P:(dc + 1) * P], GX[g % 3][:, dc * P:(dc + 1) * P], ident), mark=dc == DC - 1)
                gx_free[g % 3] = [tr]
                src = bank[bk][:, 0:D].rearrange("p (a b) -> p a b", a=DC)
                if layer == 0:
                    st["xs", g] = copy_on(act, [tr, *xs_free[j]], xsT[j], src)
                    free[bk] = [st["xs", g]]
                else:
                    st["xs", g] = split(tr, *xsT[j], src, [bk], xs_free[j])
                gather_to(g + 4)

            def up_banks(g):
                if layer == 0:
                    k = 2 * (g % 2)
                    return [k, k + 1], bank[k], bank[k + 1]
                return [g % 4], bank[g % 4][:, 0:F], bank[g % 4][:, F:2 * F]

            def up(g):
                j, (bks, gate, _) = g % 3, up_banks(g)

                def columns(w, dc, n):
                    return w[:, dc, bass.ds(expert[g] * (2 * F) + n * 512, 512)]

                ms = []
                for n in range(len(bks)):
                    waits = [st["xs", g], ex_done, *w1_ready, *free[bks[n]]]
                    for dc in range(DC):
                        if layer == 0:
                            mm = pe.add(waits, lambda e, n=n, dc=dc: e.matmul(
                                bank[bks[n]], xsT[j][:, dc, :], columns(W1, dc, n),
                                start=(dc == 0), stop=(dc == DC - 1)), mark=dc == DC - 1)
                        else:
                            xh, xl = (v_[:, dc, :] for v_ in xsT[j])
                            for m, (x_, w_) in enumerate(((xh, 0), (xh, 1), (xl, 0))):
                                last = dc == DC - 1 and m == 2
                                mm = pe.add(waits, lambda e, dc=dc, m=m, x_=x_, w_=w_, last=last: e.matmul(
                                    bank[bks[0]], x_, columns(W1[w_], dc, 0), start=(dc == 0 and m == 0),
                                    stop=last), mark=last)
                    ms.append(mm)
                xs_free[j] = [mm]
                st["up", g] = ms
                if layer == 1:
                    u = G2[g % NH_]
                    a = act.add([ms[0], *h_free[g % NH_]], lambda e: e.activation(u, gate, ACT.Square))
                    a = dve.add([a], lambda e: e.tensor_scalar(
                        u, u, GELU_C * 0.044715, GELU_C, ALU.mult, ALU.add))
                    st["inner", g] = dve.add([a], lambda e: e.tensor_tensor(u, gate, u, ALU.mult))

            def activate(g):
                bks, gate, upv = up_banks(g)
                ms, h = st["up", g], H[g % NH_]
                if layer == 0:
                    a = act.add([ms[0], *h_free[g % NH_]], lambda e: e.activation(h, gate, ACT.Tanh, scale=0.5))
                else:
                    u = G2[g % NH_]
                    a = act.add([st["inner", g], *h_free[g % NH_]], lambda e: e.activation(h, u, ACT.Tanh))
                a = dve.add([a], lambda e: e.scalar_tensor_tensor(h, h, 1.0, gate, ALU.add, ALU.mult))
                a = dve.add([a, ms[-1]], lambda e: e.scalar_tensor_tensor(h, h, 0.5, upv, ALU.mult, ALU.mult))
                st["h", g] = a
                for b in bks:
                    free[b] = [a]

            def turn_h(g):
                j, bk, h = g % 2, 5 + g % 2, H[g % NH_]
                for ic in range(IC):
                    tr = pe.add([st["h", g], *free[bk]], lambda e, ic=ic: e.transpose(
                        bank[bk][:, ic * P:(ic + 1) * P], h[:, ic * P:(ic + 1) * P], ident), mark=ic == IC - 1)
                h_free[g % NH_] = [tr]
                st["ht", g] = copy_on(act, [tr, *ht_free[j]], HT[j],
                                      bank[bk][:, 0:F].rearrange("p (a b) -> p a b", a=IC))
                free[bk] = [st["ht", g]]

            def down(g):
                j, bk = g % 2, 7

                def one(e, ic):
                    return e.matmul(bank[bk][:, 0:D], HT[j][:, ic, :], W2[:, ic, bass.ds(expert[g] * D, D)],
                                    start=(ic == 0), stop=(ic == IC - 1))

                for ic in range(IC):
                    mm = pe.add([st["ht", g], *w2_ready, *free[bk]], lambda e, ic=ic: one(e, ic), mark=ic == IC - 1)
                ht_free[j] = [mm]
                zc = copy_on(dve, [mm, *z_free[j]], Z[j], bank[bk][:, 0:D])
                free[bk] = [zc]
                z_free[j] = [sp.dma([zc, *spare_rows], lambda e: e.dma_start(ys_dram[layer][g * P:(g + 1) * P, :], Z[j]),
                                    z_sem[layer][j + (2 if g >= NM else 0)])]
                st["down"] = mm

            def tiles(lo, hi, meanwhile=lambda: None):
                st["end"] = hi
                gather_to(lo + 3)
                load_expert(lo)
                turn_x(lo)
                for g in range(lo, lo + AH):
                    load_expert(g + 1)
                    turn_x(g + 1)
                    up(g)
                    if layer == 0 or g > lo:
                        activate(g if layer == 0 else g - 1)
                if lo + AH + 1 < hi:
                    load_expert(lo + AH + 1)
                    turn_x(lo + AH + 1)
                for g in range(lo, hi):
                    if g + AH < hi:
                        up(g + AH)
                    if g + 1 < hi:
                        activate(g + 1)
                    if g + AH + 2 < hi:
                        load_expert(g + AH + 2)
                    turn_h(g)
                    if g + AH + 2 < hi:
                        turn_x(g + AH + 2)
                    if g > lo:
                        down(g - 1)
                    if g == lo + 4:
                        meanwhile()
                down(hi - 1)

            tiles(0, NM, during)
            for q in (pe, act, dve, pool, sp):
                q.begin_if_more([ex_done], tiles_of[0:1, 0:1], NM)
            tiles(NM, NT)
            more_stored = sp.add([z_sem[layer][i].token() for i in (2, 3)], lambda e: e.nop())
            for q in (pe, act, dve, pool, sp):
                q.end_if()
            return xs_free[(NT - 1) % 3][0], st["down"], [*(z_sem[layer][i].token() for i in (0, 1)), more_stored, *spare_rows]

        YG = view(R2, 0, [TOPK * TT, D])
        yg_sem = [[counter(f"yg{l}_{c}") for c in range(TOPK * TT)] for l in range(2)]

        def combine(layer, z_tokens, slot_done, w_done, r2_free, finish, apply=lambda i: None):
            toks = {}

            def gather(i):
                for k in range(TOPK):
                    c = k * TT + i
                    toks[i, k] = pool.dma([*z_tokens, slot_done, *r2_free], lambda e, c=c: e.indirect_dma_start(
                        YG[:, c, :], None, ys_dram[layer], bass.IndirectOffsetOnAxis(slot_of[:, c:c + 1], 0)),
                        yg_sem[layer][c])

            def tile(i):
                tk = w_done
                for k in range(TOPK):
                    c = k * TT + i
                    tk = dve.add([toks[i, k], tk], lambda e, c=c, k=k: e.scalar_tensor_tensor(
                        X[:, i, :], YG[:, c, :], wts[:, k, i:i + 1], X[:, i, :], ALU.mult, ALU.add))
                finish(i, tk)
                if layer == 1 and i + 4 < TT:
                    gather(i + 4)
                if i % 4:
                    apply(i - 1)
                if i % 4 == 3:
                    apply(i)

            for i in range(4):
                gather(i)
            tile.gather = gather
            return tile

        store_sem = [[counter(f"store{l}_{i}") for i in range(TT)] for l in range(2)]

        def tile_steps(layer, rt, xn_free, xnT_free):
            stored, stats, normed, turned, factor = [], {}, {}, {}, {}

            def finish(i, x_ready):
                stats[i] = norm_stats(i, [x_ready])

            def apply(i):
                normed[i] = norm_apply(i, stats[i], xn_free)
                stored.append(sp.dma([normed[i]], lambda e: e.dma_start(
                    xn_dram[layer][i * P:(i + 1) * P, :], XN[:, i, :]), store_sem[layer][i]))

            def turn(i):
                tr, src = transpose_xn(i, 1, normed[i])
                turned[i] = copy_on(act, [tr, *xnT_free], xnT[:, :, i * P:(i + 1) * P], src)
                free[1] = [turned[i]]
                if layer == 1:
                    factor[i] = router_factor(i, normed[i], rt)

            def route(i):
                route_tile(layer, i, turned[i], factor.get(i), rt)

            return stored, finish, apply, turn, route

        rt0 = {"lg_free": [], "junk_free": []}
        w2 = view(R2, 0, [F0 // P, NE, D])
        ld_w2 = []

        def load_w2(i):
            if i in (3, 7):
                n = i // 4
                ld_w2.append(load(f"ld_w2_{n}", w2[:, 2 * n:2 * n + 2, :, :], t["w2"][:, 2 * n:2 * n + 2, :, :],
                                  [at0.q_done[i]]))

        stored0, *steps0 = tile_steps(0, rt0, [], [q0_last_mm])
        ckv1, wo1 = view(R4, 8, [NH, C]), view(R4, 12, [NH, D])
        ld_ckv1 = load("ld_ckv1", ckv1, t["ckv1"], [q0_last_mm])
        ld_wo1 = load("ld_wo1", wo1, t["wo1"], [q0_last_mm])
        at0.run(b_ready, *steps0, each=load_w2)
        tok_done, ex_done, slot_done, weigh0 = route(
            0, rt0["sorted"], lambda: output_matrices(ckv1, wo1, [ld_ckv1, ld_wo1], [at0.b_done], (act, act)))
        b1_ready, raw1_done = rt_extra[-1]
        w1f = view(R1, 0, [DC, NE * 2 * F0])
        w2f = view(R2, 0, [F0 // P, NE * D])

        r4_free = [rt0["sorted"], q0_last_mm, raw1_done]
        wq1, kcq1 = view(R4, 0, [NH, D]), view(R4, 16, [NH, QW])
        ld_raw1 = []

        w_done = []

        def during_experts0():
            w_done.append(weigh0())
            ld_raw1.append(load("ld_wq1", wq1, t["wq1"], r4_free))
            ld_raw1.append(load("ld_kcq1", kcq1, t["kcq1"], r4_free))

        up_done, down_done, z_tok = experts(0, w1f, w2f, F0, ld_w1, ld_w2, stored0, tok_done, ex_done,
                                            [at0.b_done, rt0["sorted"]], during_experts0)
        rt_free["exp"] = [down_done]

        NBK = 3
        CMH, CML = (v_[:, :].rearrange("p (a b c) -> p a b c", a=DC, b=NP) for v_ in (CMH_, CML_))
        TTm = view(R1, 48, [NP, NBK, P])
        qr1, kr1 = view(R2, 16, [NP, NBK * P]), view(R2, 28, [NP, P])
        ld_qr1 = load("ld_qr1", qr1, t["qr1"], [down_done])
        ld_kr1 = load("ld_kr1", kr1, t["kr1"], [down_done])

        def expand_matrices(between):
            toks = []
            for hp in range(NP):
                for dc in range(DC):
                    bk = (2 * hp + dc) % 4
                    wq_ = [wq1[:, 2 * hp + h2, dc * P:(dc + 1) * P] for h2 in range(2)]
                    k0, k1 = kcq1[:, 2 * hp, :], kcq1[:, 2 * hp + 1, :]
                    for out_, w_, x_ in (
                            (bank[bk].rearrange("p (a b) -> p a b", a=2)[:, :, 0:HQ], wq_[0],
                             k0.rearrange("p (a b) -> p a b", a=2)),
                            (bank[bk][:, HQ:2 * P], wq_[1], k1[:, 0:2 * P - HQ]),
                            (bank[bk][:, 2 * P + HQ:3 * P], wq_[1], k1[:, 2 * P - HQ:])):
                        mm = pe.add([*ld_raw1, *free[bk]], lambda e, out_=out_, w_=w_, x_=x_: e.matmul(
                            out_, w_, x_, start=True, stop=True))
                    toks.append(split(mm, CMH[:, dc, hp, :], CML[:, dc, hp, :], bank[bk][:, 0:3 * P], [bk], [up_done]))
                between(hp)
            return toks

        def latent_matrices(between):
            toks = []
            for p in range(NP):
                bk = p % 6
                for j in range(NBK):
                    mm = pe.add([ld_qr1, ld_kr1, *free[bk]], lambda e, bk=bk, j=j, p=p: e.matmul(
                        bank[bk][:, j * P:(j + 1) * P], qr1[:, p, j * P:(j + 1) * P], kr1[:, p, :],
                        start=True, stop=True), mark=j == NBK - 1)
                tk = copy_on(act, [mm, up_done], TTm[:, p, :, :],
                             bank[bk][:, 0:NBK * P].rearrange("p (a b) -> p a b", a=NBK))
                free[bk] = [tk]
                toks.append(tk)
                between(p)
            return toks

        xnT1_ready, stats1, normed1 = {}, {}, {}

        def norm1_finish(i, x_ready):
            stats1[i] = norm_stats(i, [x_ready])

        def norm1_apply(i):
            normed1[i] = norm_apply(i, stats1[i], stored0)

        def turn_norm1(i):
            xnT1_ready[i] = split_xn(i, 6 + i % 2, normed1[i], [cm_ready[-1]])

        combine_tile = combine(0, z_tok, slot_done, w_done[0], [down_done], norm1_finish, norm1_apply)
        cm_ready = expand_matrices(lambda hp: combine_tile(hp - 4) if 4 <= hp < 8 else None)
        tt_ready = latent_matrices(lambda p: turn_norm1({p: i for i, p in enumerate(())}[p]) if p in () else None)
        turn_norm1(0)
        turn_norm1(1)
        turn_norm1(2)
        turn_norm1(3)

        RO = [view(R4, 16 + 6 * i, [NBK, 512]) for i in range(2)]
        PR = [view(R3, 8 + 6 * i, [NBK, 512]) for i in range(2)]
        pr_free = [list(b1_ready) + z_tok for _ in range(2)]
        ro_free = [[cm_ready[-1]] for _ in range(2)]
        q1_ready = {}
        LO, HI = slice(0, 64), slice(64, 128)

        def v3(ap):
            return ap.rearrange("p (a b) -> p a b", b=S)

        def tab(v, rows=slice(0, P)):
            return bc(ropeq[rows, v, :], 8)

        def roped_pair(n, hf, p):
            bks, ro, pr = [3 * (n % 2) + j for j in range(NBK)], RO[n % 2], PR[n % 2]
            mms = {}
            for j in (0, 2, 1):
                rows, cols = slice(j * P, (j + 1) * P), slice(hf * 512, (hf + 1) * 512)
                for dc in range(DC):
                    mm = product(bank[bks[j]], CMH[:, dc, p, rows], CML[:, dc, p, rows],
                                 XH[:, dc, cols], XL[:, dc, cols],
                                 [*cm_ready, *[xnT1_ready[i] for i in range(4 * hf, 4 * hf + 4)], *free[bks[j]]],
                                 dc == 0, dc == DC - 1)
                mms[j] = mm
            ALL = slice(0, P)
            for src, rs_, v, dst, rd in ((0, ALL, 0, ro[:, 0, :], ALL), (0, ALL, 3, pr[:, 2, :], ALL),
                                         (2, ALL, 1, pr[:, 0, :], ALL), (2, ALL, 2, ro[:, 2, :], ALL),
                                         (1, ALL, 4, ro[:, 1, :], ALL), (1, HI, 5, pr[:, 1, :], LO),
                                         (1, LO, 5, pr[:, 1, :], HI)):
                tk = dve.add([mms[src], ld_ropeq, *pr_free[n % 2], *ro_free[n % 2]],
                             lambda e, src=src, rs_=rs_, v=v, dst=dst, rd=rd: e.tensor_tensor(
                                 v3(dst[rd]), v3(bank[bks[src]][rs_]), tab(v, rs_), ALU.mult))
                free[bks[src]] = [tk]
            for j in (0, 2, 1):
                r = pool.add([tk], lambda e, j=j: e.tensor_tensor(ro[:, j, :], ro[:, j, :], pr[:, j, :], ALU.add))
            pr_free[n % 2] = [r]
            return r

        def latent_query(n, hf, p, roped):
            bk = 6 + n % 2
            for m, j in enumerate((0, 2, 1)):
                mm = pe.add([roped, *tt_ready, *free[bk]], lambda e, j=j, m=m: e.matmul(
                    bank[bk], TTm[:, p, j, :], RO[n % 2][:, j, :], start=(m == 0), stop=(m == 2)), mark=m == 2)
            q1_ready[p, hf] = copy_on(act, [mm, q_free], Q[:, hf, p, :], bank[bk])
            free[bk] = [q1_ready[p, hf]]
            ro_free[n % 2] = [mm]

        at1 = Attention(lambda i: [q1_ready[p, i // 4] for p in range(NP)], [b1_ready[-1], *z_tok])
        n, todo = 0, []
        for hf in range(2):
            for p in range(NP):
                if hf == 0 and p < 4:
                    combine_tile.gather(4 + p)
                todo.append((n, hf, p, roped_pair(n, hf, p)))
                if hf == 0 and 1 <= p < 5:
                    combine_tile(3 + p)
                    q_free = (dve.sem, dve.count)
                if hf == 0 and p >= 4:
                    turn_norm1(p)
                if len(todo) == 2:
                    latent_query(*todo.pop(0))
                n += 1
                if (hf, p) == (1, 1):
                    at1.scores(0, 3, range(NP - 1, -1, -1))
                    at1.exponential(0)
                if (hf, p) == (1, 2):
                    at1.normalise(0)
                if (hf, p) == (1, 4):
                    at1.scores(1, 3)
                    at1.exponential(1)
                if (hf, p) == (1, 5):
                    at1.normalise(1)
        latent_query(*todo.pop(0))

        rope_done = (pe.sem, pe.count)
        G1H, G1L = (v_[:, :].rearrange("p (a b) -> p a b", a=DC) for v_ in (G1H_, G1L_))
        g1_raw = view(R1, 32, [DC * NE * 2 * F1])
        l1 = view(R4, 8, [F1 // P, NE * D])
        NCH = 8
        CHW = DC * NE * 2 * F1 // NCH
        ld_g1 = [load(f"ld_g1_{i}", g1_raw[:, i * CHW:(i + 1) * CHW], t["g1"][:, i * CHW:(i + 1) * CHW], [rope_done])
                 for i in range(NCH)]
        ld_l1 = [load("ld_l1", l1, t["l1"], [rope_done])]
        g1_ready = []

        def split_g1(chunks):
            for c in chunks:
                cols = slice(c * CHW, (c + 1) * CHW)
                a = act.add([ld_g1[c]], lambda e, cols=cols: e.copy(G1H_[:, cols], g1_raw[:, cols]))
                g1_ready.append(pool.add([a], lambda e, cols=cols: e.tensor_tensor(
                    G1L_[:, cols], g1_raw[:, cols], G1H_[:, cols].bitcast(F32), ALU.subtract)))

        rt1 = {"lg_free": [ex_done], "junk_free": []}
        for k in range(2):
            at1.et_free[k] = at1.ct_free[k] = [(pool.sem, pool.count), (dve.sem, dve.count)]
        stored1, *steps1 = tile_steps(1, rt1, [], [rope_done])
        at1.run(b1_ready, *steps1, each=lambda i: split_g1([i - 3] if 3 <= i < 8 else []))
        tok1, ex1, slot1, weigh1 = route(1, rt1["sorted"], lambda: split_g1(range(5, NCH)))
        up1, down1, z1 = experts(1, (G1H, G1L), l1, F1, g1_ready, ld_l1, stored1, tok1, ex1,
                                 [at1.b_done, rt1["sorted"], (act.sem, act.count)],
                                 lambda: w_done.append(weigh1()))
        out_sem = counter("out")

        def write_out(i, x_ready):
            sp.dma([x_ready], lambda e: e.dma_start(out[i * P:(i + 1) * P, :], X[:, i, :]), out_sem)

        combine_tile = combine(1, z1, slot1, w_done[1], [at1.q_done[TT - 1]], write_out)
        for i in range(TT):
            combine_tile(i)

        block = ctx.enter_context(nc.Block())

        @block.sync
        def _(e):
            sp.play(e)
            e.wait_ge(out_sem.sem, out_sem.count)

        @block.scalar
        def _(e):
            act.play(e)

        @block.vector
        def _(e):
            dve.play(e)

        @block.gpsimd
        def _(e):
            pool.play(e)

        @block.tensor
        def _(e):
            pe.play(e)


def tables():
    f = np.float32
    k, m = np.arange(P)[:, None], np.arange(P)[None, :]
    consts = np.stack([(k == m), (k < m), np.ones((P, P))], 1).astype(f)

    def rope(n, dim):
        inv = f(1.0) / np.power(f(10000.0), np.arange(0, dim, 2, dtype=f) / f(dim)).astype(f)
        fr = np.arange(n, dtype=f)[:, None] * inv[None, :]
        return np.repeat(np.sin(fr), 2, -1).astype(f), np.repeat(np.cos(fr), 2, -1).astype(f)

    sin, cos = rope(S, C)
    sign = np.where(np.arange(C) < C // 2, f(-1), f(1))
    ropek = np.concatenate([np.stack([cos, sin * sign], 1)] * 2, 0)
    sin, cos = rope(S, QW)
    q = np.arange(P) % HQ
    q1 = HQ - 64 + np.arange(64)
    ropeq = np.stack([cos[:, q].T, -sin[:, q].T, cos[:, q + HQ].T, sin[:, q + HQ].T,
                      np.concatenate([cos[:, q1].T, cos[:, q1 + HQ].T]),
                      np.concatenate([sin[:, q1 + HQ].T, -sin[:, q1].T])], 1)
    small = np.zeros((P, 256), f)
    small[:, 0:8] = np.arange(8)
    small[:, 8:136] = np.arange(P)
    small[:, 136:152] = np.tile(np.arange(TT), TOPK)
    small[:, 152:216] = (np.arange(8)[None, :] < np.arange(8)[:, None]).reshape(-1)
    small[:, 216:216 + NT] = np.arange(NT)
    small[:, 248] = np.arange(P)
    return {"consts": consts, "ropek": ropek, "ropeq": ropeq, "small": small}


def lay_out(i):
    a = {"x": i["x"].reshape(TT, P, D).transpose(1, 0, 2), "ctx": i["ctx_512"].transpose(1, 0, 2)}
    for l in range(2):
        def w(n):
            return i[f"L{l}_xattn_{n}"]
        kr = w("W_kr").reshape(NP, 2, C, 64).transpose(1, 3, 0, 2)
        a[f"kr{l}"] = np.zeros((P, NP, P), kr.dtype)
        for par in range(2):
            a[f"kr{l}"][64 * par:64 * par + 64, :, 64 * par:64 * par + 64] = kr[par]
        a[f"wq{l}"] = w("Wq").reshape(NH, HK, D).transpose(1, 0, 2)
        a[f"ckv{l}"] = w("w_kc_kv").transpose(1, 0, 2)
        a[f"wo{l}"] = w("Wo").reshape(D, NH, HK).transpose(2, 1, 0)
    a["kcq0"] = i["L0_xattn_w_kc_q"].reshape(NH, HK, 2, HQ).transpose(3, 2, 0, 1)
    qr0, qr1 = (i[f"L{l}_xattn_W_qr"].reshape(NP, 2, QW, 64).transpose(1, 3, 0, 2) for l in range(2))
    a["qr0"] = qr0.reshape(P, NP, QW)
    cut = P - HQ
    a["qr1"] = np.zeros((P, NP, 3 * P), qr1.dtype)
    a["qr1"][0:64, :, 0:HQ], a["qr1"][0:64, :, 2 * P:2 * P + HQ] = qr1[0][..., 0:HQ], qr1[0][..., HQ:QW]
    a["qr1"][64:, :, HQ:P], a["qr1"][64:, :, 2 * P + HQ:] = qr1[1][..., 0:cut], qr1[1][..., HQ:HQ + cut]
    a["qr1"][64:, :, P:P + 64], a["qr1"][64:, :, P + 64:2 * P] = qr1[1][..., cut:HQ], qr1[1][..., HQ + cut:]
    kcq1 = i["L1_xattn_w_kc_q"].transpose(1, 0, 2)
    a["kcq1"] = kcq1.copy()
    odd = kcq1[:, 1::2]
    a["kcq1"][:, 1::2] = np.concatenate(
        [odd[..., 0:cut], odd[..., cut:HQ], odd[..., HQ + cut:], odd[..., HQ:HQ + cut]], -1)
    a["w1"] = i["L0_ffn_w1"].reshape(NE, 2 * F0, DC, P).transpose(3, 2, 0, 1)
    a["w2"] = i["L0_ffn_w2"].reshape(NE, D, F0 // P, P).transpose(3, 2, 0, 1)
    a["g1"] = i["L1_ffn_gating_einsum"].reshape(NE, 2 * F1, DC, P).transpose(3, 2, 0, 1).reshape(P, DC * NE * 2 * F1)
    a["l1"] = i["L1_ffn_linear"].reshape(NE, F1 // P, P, D).transpose(2, 1, 0, 3).reshape(P, F1 // P, NE * D)
    a["rout"] = np.stack([i["L0_ffn_router_w"].reshape(NE, DC, P).transpose(2, 1, 0),
                          i["L1_ffn_router_logits"].reshape(DC, P, NE).transpose(1, 0, 2)], 1)
    a["rscale"] = i["L1_ffn_router_scale"].reshape(DC, P).T
    a["pes"] = np.broadcast_to(i["L1_ffn_per_expert_scale"], (P, NE))
    return a


def kernel(**inputs):
    import concourse.bacc as _bacc
    from concourse.bass_utils import run_bass_kernel_spmd as _run

    nc = _bacc.Bacc("TRN2", target_bir_lowering=False, num_devices=1)
    arrays, aps = {}, {}
    for name, a in {**lay_out({k: np.asarray(v) for k, v in inputs.items()}), **tables()}.items():
        arrays[f"in_{name}"] = np.ascontiguousarray(a)
        aps[name] = nc.dram_tensor(f"in_{name}", a.shape, mybir.dt.from_np(a.dtype), kind="ExternalInput").ap()
    out = nc.dram_tensor("out", [TOK, D], F32, kind="ExternalOutput").ap()
    build(nc, aps, out)
    r = _run(nc, [arrays], core_ids=[0])
    return r.results[0]["out"].reshape(NB, S, D)
```
